# Optimizing a Trainium2 kernel written in Bass

```python
import numpy as np
import jax
import jax.numpy as jnp

def _softmax(x, axis=-1):
    return jax.nn.softmax(x, axis=axis)

def _gelu(x):
    return jax.nn.gelu(x, approximate=True)

def _silu(x):
    return jax.nn.silu(x)

def _sigmoid(x):
    return jax.nn.sigmoid(x)

def _layernorm(x, axis=-1, eps=1e-05):
    m = jnp.mean(x, axis=axis, keepdims=True)
    v = jnp.var(x, axis=axis, keepdims=True)
    return (x - m) / jnp.sqrt(v + eps)

def _scatter_add(tgt, idx, src, axis=0):
    return tgt.at[idx].add(src)

def _segment_sum(src, seg, n):
    return jax.ops.segment_sum(src, seg, n)
kernel_name = 'mk_macaron_d2_jaxref_r4_ec8724'

def setup_inputs(seed: int=0):
    np.random.seed(seed)
    _w = jnp.asarray

    def _L0_attn_setup():
        import jax, jax.numpy as jnp
        import numpy as np
        D_MODEL = 256
        D_INNER = 512
        N_STATES = 16
        DT_RANK = 64
        K = 4
        B_SZ = 2
        L = 512

        def _causal_conv(x, w):
            xt = jnp.transpose(x, (0, 2, 1))
            y = jax.lax.conv_general_dilated(xt, w, window_strides=(1,), padding=[(K - 1, 0)], feature_group_count=D_INNER, dimension_numbers=('NCH', 'OIH', 'NCH'))
            return jnp.transpose(y, (0, 2, 1))

        def _selective_scan(delta, A, Bmat, C, x):
            dA = jnp.exp(delta[..., None] * A[None, None])
            dBx = (delta * x)[..., None] * Bmat[:, :, None, :]

            def step(h, inputs):
                dA_t, dBx_t = inputs
                h = dA_t * h + dBx_t
                y = jnp.einsum('bdn,dn->bd', h, C)
                return (h, y)
            h0 = jnp.zeros((x.shape[0], D_INNER, N_STATES), x.dtype)
            _, ys = jax.lax.scan(step, h0, (jnp.moveaxis(dA, 1, 0), jnp.moveaxis(dBx, 1, 0)))
            return jnp.moveaxis(ys, 0, 1)
        key = jax.random.key(seed)
        ks = jax.random.split(key, 10)
        inp = {}
        inp['input'] = jax.random.normal(ks[0], (B_SZ, L, D_MODEL), jnp.float32)
        out_dim = 2 * D_INNER + N_STATES + DT_RANK
        inp['Win'] = jax.random.normal(ks[1], (out_dim, D_MODEL), jnp.float32) * 0.02
        inp['b_in'] = jnp.zeros((out_dim,), jnp.float32)
        inp['A_log'] = jnp.log(jnp.tile(jnp.arange(1, N_STATES + 1, dtype=jnp.float32), (D_INNER, 1)))
        inp['B_param'] = jax.random.normal(ks[2], (N_STATES,), jnp.float32) / N_STATES ** 0.5
        inp['C_param'] = jax.random.normal(ks[3], (D_INNER, N_STATES), jnp.float32) / N_STATES ** 0.5
        inp['Wdt'] = jax.random.normal(ks[4], (D_INNER, DT_RANK), jnp.float32) * 0.02
        dt_vals = jnp.exp(jax.random.uniform(ks[5], (D_INNER,), jnp.float32) * (np.log(0.1) - np.log(0.001)) + np.log(0.001))
        inp['b_dt'] = jnp.log(jnp.expm1(dt_vals))
        inp['Wconv'] = jax.random.normal(ks[6], (D_INNER, 1, K), jnp.float32) * (1.0 / np.sqrt(K))
        inp['Wout'] = jax.random.normal(ks[7], (D_MODEL, D_INNER), jnp.float32) * 0.02
        inp['b_out'] = jnp.zeros((D_MODEL,), jnp.float32)
        return inp
    _L0_attn_in = _L0_attn_setup()

    def _L0_ffn_setup():
        import jax, jax.numpy as jnp
        import numpy as np
        B, S, H = (4, 512, 256)
        E, K, INTER = (16, 2, 128)
        ALPHA, LIMIT = (1.702, 7.0)
        key = jax.random.key(seed)
        ks = jax.random.split(key, 6)
        return {'hidden_states': jax.random.normal(ks[0], (B, S, H), jnp.float32), 'router_weight': jax.random.normal(ks[1], (H, E), jnp.float32) * 0.02, 'gate_up_proj': jax.random.normal(ks[2], (E, H, 2 * INTER), jnp.float32) * 0.02, 'gate_up_proj_bias': jax.random.normal(ks[3], (E, 2 * INTER), jnp.float32) * 0.02, 'down_proj': jax.random.normal(ks[4], (E, INTER, H), jnp.float32) * 0.02, 'down_proj_bias': jax.random.normal(ks[5], (E, H), jnp.float32) * 0.02}
    _L0_ffn_in = _L0_ffn_setup()

    def _L1_attn_setup():
        import jax, jax.numpy as jnp
        import numpy as np
        B, S, D, H = (2, 512, 256, 16)
        HD = D // H
        key = jax.random.key(seed)
        ks = jax.random.split(key, 5)
        scale = 1.0 / np.sqrt(D)
        x = jax.random.normal(ks[0], (B, S, D), dtype=jnp.float32)
        W_Q = jax.random.uniform(ks[1], (D, D), jnp.float32, -scale, scale)
        W_K = jax.random.uniform(ks[2], (D, D), jnp.float32, -scale, scale)
        W_V = jax.random.uniform(ks[3], (D, D), jnp.float32, -scale, scale)
        W_O = jax.random.uniform(ks[4], (D, D), jnp.float32, -scale, scale)
        return {'x': x, 'W_Q': W_Q, 'W_K': W_K, 'W_V': W_V, 'W_O': W_O}
    _L1_attn_in = _L1_attn_setup()

    def _L1_ffn_setup():
        import jax, jax.numpy as jnp
        import numpy as np
        B, S, D = (2, 256, 256)
        E, K, F, FS = (8, 2, 128, 256)
        key = jax.random.key(seed)
        ks = jax.random.split(key, 9)
        s = lambda k, shape, fan: jax.random.normal(k, shape, jnp.float32) * fan ** (-0.5)
        return {'x': jax.random.normal(ks[0], (B, S, D), jnp.float32), 'Wr': s(ks[1], (D, E), D), 'Wg': s(ks[2], (E, D, F), D), 'Wu': s(ks[3], (E, D, F), D), 'Wd': s(ks[4], (E, F, D), F), 'Sg': s(ks[5], (D, FS), D), 'Su': s(ks[6], (D, FS), D), 'Sd': s(ks[7], (FS, D), FS), 'expert_bias': jnp.zeros((E,), jnp.float32)}
    _L1_ffn_in = _L1_ffn_setup()
    _d = {'L0_attn_input': _L0_attn_in['input'], 'L0_attn_Win': _L0_attn_in['Win'], 'L0_attn_b_in': _L0_attn_in['b_in'], 'L0_attn_A_log': _L0_attn_in['A_log'], 'L0_attn_B_param': _L0_attn_in['B_param'], 'L0_attn_C_param': _L0_attn_in['C_param'], 'L0_attn_Wdt': _L0_attn_in['Wdt'], 'L0_attn_b_dt': _L0_attn_in['b_dt'], 'L0_attn_Wconv': _L0_attn_in['Wconv'], 'L0_attn_Wout': _L0_attn_in['Wout'], 'L0_attn_b_out': _L0_attn_in['b_out'], 'L0_ffn_router_weight': _L0_ffn_in['router_weight'], 'L0_ffn_gate_up_proj': _L0_ffn_in['gate_up_proj'], 'L0_ffn_gate_up_proj_bias': _L0_ffn_in['gate_up_proj_bias'], 'L0_ffn_down_proj': _L0_ffn_in['down_proj'], 'L0_ffn_down_proj_bias': _L0_ffn_in['down_proj_bias'], 'L1_attn_W_Q': _L1_attn_in['W_Q'], 'L1_attn_W_K': _L1_attn_in['W_K'], 'L1_attn_W_V': _L1_attn_in['W_V'], 'L1_attn_W_O': _L1_attn_in['W_O'], 'L1_ffn_Wr': _L1_ffn_in['Wr'], 'L1_ffn_Wg': _L1_ffn_in['Wg'], 'L1_ffn_Wu': _L1_ffn_in['Wu'], 'L1_ffn_Wd': _L1_ffn_in['Wd'], 'L1_ffn_Sg': _L1_ffn_in['Sg'], 'L1_ffn_Su': _L1_ffn_in['Su'], 'L1_ffn_Sd': _L1_ffn_in['Sd'], 'L1_ffn_expert_bias': _L1_ffn_in['expert_bias']}
    _x0 = _d['L0_attn_input']
    _d['L0_attn_input'] = jax.random.normal(jax.random.fold_in(jax.random.key(seed), 1), (8, 512, 256), dtype=_x0.dtype)
    del _x0
    return _d

def reference(L0_attn_input, L0_attn_Win, L0_attn_b_in, L0_attn_A_log, L0_attn_B_param, L0_attn_C_param, L0_attn_Wdt, L0_attn_b_dt, L0_attn_Wconv, L0_attn_Wout, L0_attn_b_out, L0_ffn_router_weight, L0_ffn_gate_up_proj, L0_ffn_gate_up_proj_bias, L0_ffn_down_proj, L0_ffn_down_proj_bias, L1_attn_W_Q, L1_attn_W_K, L1_attn_W_V, L1_attn_W_O, L1_ffn_Wr, L1_ffn_Wg, L1_ffn_Wu, L1_ffn_Wd, L1_ffn_Sg, L1_ffn_Su, L1_ffn_Sd, L1_ffn_expert_bias):

    def _L0_attn_ref(input, Win, b_in, A_log, B_param, C_param, Wdt, b_dt, Wconv, Wout, b_out):
        import jax, jax.numpy as jnp
        import numpy as np
        D_MODEL = 256
        D_INNER = 512
        N_STATES = 16
        DT_RANK = 64
        K = 4
        B_SZ = 2
        L = 512

        def _causal_conv(x, w):
            xt = jnp.transpose(x, (0, 2, 1))
            y = jax.lax.conv_general_dilated(xt, w, window_strides=(1,), padding=[(K - 1, 0)], feature_group_count=D_INNER, dimension_numbers=('NCH', 'OIH', 'NCH'))
            return jnp.transpose(y, (0, 2, 1))

        def _selective_scan(delta, A, Bmat, C, x):
            dA = jnp.exp(delta[..., None] * A[None, None])
            dBx = (delta * x)[..., None] * Bmat[:, :, None, :]

            def step(h, inputs):
                dA_t, dBx_t = inputs
                h = dA_t * h + dBx_t
                y = jnp.einsum('bdn,dn->bd', h, C)
                return (h, y)
            h0 = jnp.zeros((x.shape[0], D_INNER, N_STATES), x.dtype)
            _, ys = jax.lax.scan(step, h0, (jnp.moveaxis(dA, 1, 0), jnp.moveaxis(dBx, 1, 0)))
            return jnp.moveaxis(ys, 0, 1)
        xp = input @ Win.T + b_in
        v, x, Bproj, dr = jnp.split(xp, [D_INNER, 2 * D_INNER, 2 * D_INNER + N_STATES], axis=-1)
        x = jax.nn.silu(_causal_conv(x, Wconv))
        delta = jax.nn.softplus(dr @ Wdt.T + b_dt)
        A = -jnp.exp(A_log)
        Bmat = Bproj + B_param[None, None, :]
        y = _selective_scan(delta, A, Bmat, C_param, x)
        out = y * jax.nn.silu(v)
        return out @ Wout.T + b_out

    def _L0_ffn_ref(hidden_states, router_weight, gate_up_proj, gate_up_proj_bias, down_proj, down_proj_bias):
        import jax, jax.numpy as jnp
        import numpy as np
        B, S, H = (4, 512, 256)
        E, K, INTER = (16, 2, 128)
        ALPHA, LIMIT = (1.702, 7.0)
        b, s, h = hidden_states.shape
        x = hidden_states.reshape(-1, h)
        logits = x @ router_weight
        topk_w, topk_i = jax.lax.top_k(logits, K)
        topk_w = jax.nn.softmax(topk_w, axis=-1)
        one_hot = (topk_i[..., None] == jnp.arange(E)[None, None, :]).astype(topk_w.dtype)
        scores = jnp.einsum('tk,tke->te', topk_w, one_hot)
        gu = jnp.einsum('th,ehf->tef', x, gate_up_proj) + gate_up_proj_bias
        gate = gu[..., ::2]
        up = gu[..., 1::2]
        gate = jnp.minimum(gate, LIMIT)
        up = jnp.clip(up, -LIMIT, LIMIT)
        glu = gate * jax.nn.sigmoid(gate * ALPHA)
        act = (up + 1.0) * glu
        out = jnp.einsum('tei,eih,te->th', act, down_proj, scores)
        out = out + jnp.einsum('te,eh->th', scores, down_proj_bias)
        return out.reshape(b, s, h)

    def _L1_attn_ref(x, W_Q, W_K, W_V, W_O):
        import jax, jax.numpy as jnp
        import numpy as np
        B, S, D, H = (2, 512, 256, 16)
        HD = D // H
        b, s, d = x.shape
        Q = (x @ W_Q.T).reshape(b, s, H, HD).transpose(0, 2, 1, 3)
        K = (x @ W_K.T).reshape(b, s, H, HD).transpose(0, 2, 1, 3)
        V = (x @ W_V.T).reshape(b, s, H, HD).transpose(0, 2, 1, 3)
        attn = jnp.einsum('bhqd,bhkd->bhqk', Q, K) / jnp.sqrt(jnp.float32(HD))
        slopes = 1.0 / (2.0 ** 8) ** ((jnp.arange(H, dtype=jnp.float32) + 1) / H)
        pos = jnp.arange(s)
        rel = jnp.minimum(pos[None, :] - pos[:, None], 0).astype(jnp.float32)
        bias = slopes[:, None, None] * rel[None, :, :]
        causal = pos[None, :] <= pos[:, None]
        attn = jnp.where(causal[None, None], attn + bias[None], -jnp.inf)
        attn = jax.nn.softmax(attn, axis=-1)
        out = jnp.einsum('bhqk,bhkd->bhqd', attn, V)
        out = out.transpose(0, 2, 1, 3).reshape(b, s, d)
        return out @ W_O.T

    def _L1_ffn_ref(x, Wr, Wg, Wu, Wd, Sg, Su, Sd, expert_bias):
        import jax, jax.numpy as jnp
        import numpy as np
        B, S, D = (2, 256, 256)
        E, K, F, FS = (8, 2, 128, 256)
        b, s, d = x.shape
        xf = x.reshape(-1, d)
        T = xf.shape[0]
        logits = xf @ Wr + expert_bias
        top_v, top_i = jax.lax.top_k(logits, K)
        probs = jax.nn.softmax(top_v, axis=-1)
        rw = jnp.zeros_like(logits).at[jnp.arange(T)[:, None], top_i].set(probs)
        gate = jnp.einsum('td,edf->tef', xf, Wg)
        up = jnp.einsum('td,edf->tef', xf, Wu)
        h = jax.nn.silu(gate) * up
        eo = jnp.einsum('tef,efd->ted', h, Wd)
        out = jnp.einsum('te,ted->td', rw, eo)
        out = out + jax.nn.silu(xf @ Sg) * (xf @ Su) @ Sd
        return out.reshape(b, s, d)
    x = L0_attn_input
    x = x + 0.5 * _L0_ffn_ref(_layernorm(x, axis=-1), L0_ffn_router_weight, L0_ffn_gate_up_proj, L0_ffn_gate_up_proj_bias, L0_ffn_down_proj, L0_ffn_down_proj_bias)
    x = x + _L0_attn_ref(_layernorm(x, axis=-1), L0_attn_Win, L0_attn_b_in, L0_attn_A_log, L0_attn_B_param, L0_attn_C_param, L0_attn_Wdt, L0_attn_b_dt, L0_attn_Wconv, L0_attn_Wout, L0_attn_b_out)
    x = x + 0.5 * _L0_ffn_ref(_layernorm(x, axis=-1), L0_ffn_router_weight, L0_ffn_gate_up_proj, L0_ffn_gate_up_proj_bias, L0_ffn_down_proj, L0_ffn_down_proj_bias)
    x = x + 0.5 * _L1_ffn_ref(_layernorm(x, axis=-1), L1_ffn_Wr, L1_ffn_Wg, L1_ffn_Wu, L1_ffn_Wd, L1_ffn_Sg, L1_ffn_Su, L1_ffn_Sd, L1_ffn_expert_bias)
    x = x + _L1_attn_ref(_layernorm(x, axis=-1), L1_attn_W_Q, L1_attn_W_K, L1_attn_W_V, L1_attn_W_O)
    x = x + 0.5 * _L1_ffn_ref(_layernorm(x, axis=-1), L1_ffn_Wr, L1_ffn_Wg, L1_ffn_Wu, L1_ffn_Wd, L1_ffn_Sg, L1_ffn_Su, L1_ffn_Sd, L1_ffn_expert_bias)
    return x

_drawn_inputs = setup_inputs


def setup_inputs(seed=0):
    import zlib

    import numpy as np

    out = dict(_drawn_inputs(seed))
    spreads = {'L0_attn_b_in': (0.0, 0.8), 'L0_attn_b_out': (0.0, 0.8), 'L1_ffn_expert_bias': (0.0, 0.8)}
    factors = {'L0_attn_Win': 8.0,
     'L0_attn_A_log': 8.0,
     'L0_attn_B_param': 8.0,
     'L0_attn_C_param': 8.0,
     'L0_attn_Wdt': 8.0,
     'L0_attn_b_dt': 8.0,
     'L0_attn_Wconv': 8.0,
     'L0_attn_Wout': 8.0,
     'L0_ffn_gate_up_proj_bias': 21.446,
     'L0_ffn_down_proj_bias': 2.68,
     'L1_attn_W_Q': 8.0,
     'L1_attn_W_K': 8.0,
     'L1_attn_W_V': 8.0,
     'L1_attn_W_O': 8.0,
     'L1_ffn_Wr': 8.0,
     'L1_ffn_Wg': 8.0,
     'L1_ffn_Wu': 8.0,
     'L1_ffn_Wd': 8.0,
     'L1_ffn_Sg': 6.889,
     'L1_ffn_Su': 6.451,
     'L1_ffn_Sd': 6.481}
    for name, (base, spread) in spreads.items():
        noise = np.random.default_rng([zlib.crc32(name.encode()), seed]).standard_normal(out[name].shape)
        drawn = base * np.exp(spread * noise) if base else spread * noise
        out[name] = jnp.asarray(drawn.astype(out[name].dtype))
    for name, factor in factors.items():
        out[name] = (out[name] * factor).astype(out[name].dtype)
    return out
```

```python
from contextlib import ExitStack

import concourse.bass as bass
from concourse import mybir

ALU = mybir.AluOpType
ACT = mybir.ActivationFunctionType
AX = mybir.AxisListType
F32 = mybir.dt.float32
BF16 = mybir.dt.bfloat16
I32 = mybir.dt.int32
ds = bass.ds

P = 128
BATCH, SEQ, D = 8, 512, 256
T = BATCH * SEQ
NT = T // P
KD = D // P
TB = SEQ // P
EPS = 1e-5
MASKED = -1e30

F = 128
E0, E1 = 16, 8
SHARED = 256
LIMIT, ALPHA = 7.0, 1.702


def slot_tiles(experts):
    most = (2 * T - experts) // P + experts
    return most + most % 2


ROUTING = {"before": P, "ones": P, "e_less": E0, "restart": E0 * NT, "tile_start": NT,
           "j": slot_tiles(E0)}


class Chain:

    def __init__(self, eng, sem, n=0):
        self.eng, self.sem, self.n = eng, sem, n

    def step(self, ins):
        ins.then_inc(self.sem, 1)
        self.n = self.n + 1
        return self.n

    def wait(self):
        self.eng.wait_ge(self.sem, self.n)

    def link(self, ins):
        self.step(ins)
        self.wait()


def steps(eng, count, lag, body):
    first = lag + 2 + lag % 2
    last = count - count % 2
    for s in range(first):
        body(s, s % 2)
    if last > first:
        with eng.Fori(first, last - 1, 2) as i:
            body(i, 0)
            body(i + 1, 1)
    for s in range(max(last, first), count + lag):
        body(s, s % 2)


def within(s, lag, count):
    return not isinstance(s, int) or 0 <= s - lag < count


def after(j, n):
    return not isinstance(j, int) or j >= n


def bcast(ap, shape):
    return ap.broadcast_to(shape)


def layer_norm_stats(nc, dve, chain, x_sb, stats, mean, var):
    n0 = chain.n
    with dve.Fori(0, NT - 3, 4) as i:
        for u in range(4):
            dve.bn_stats(stats[:, ds(i + u, 1), :].rearrange("p a s -> p (a s)"),
                         x_sb[:, ds(i + u, 1), :].rearrange("p a d -> p (a d)")).then_inc(chain.sem, 1)
    chain.n = n0 + NT
    chain.wait()
    me, m2e, mo, m2o = (stats[:, :, k] for k in (1, 2, 4, 5))
    chain.step(dve.tensor_tensor(mean, me, mo, ALU.add))
    chain.step(dve.tensor_tensor(var, m2e, m2o, ALU.add))
    chain.link(dve.tensor_tensor(stats[:, :, 0], me, mo, ALU.subtract))
    chain.step(dve.tensor_scalar(mean, mean, 0.5, None, ALU.mult))
    chain.link(dve.tensor_tensor(stats[:, :, 3], stats[:, :, 0], stats[:, :, 0], ALU.mult))
    chain.step(dve.tensor_scalar(stats[:, :, 3], stats[:, :, 3], 0.25, EPS, ALU.mult, ALU.add))
    chain.link(dve.tensor_scalar(var, var, 1.0 / D, None, ALU.mult))
    chain.link(dve.tensor_tensor(var, var, stats[:, :, 3], ALU.add))


def layer_norm_rstd(dve, chain, var, root, rstd, scratch):
    chain.link(dve.reciprocal(rstd, root))
    chain.link(dve.tensor_tensor(scratch, rstd, rstd, ALU.mult))
    chain.link(dve.tensor_tensor(scratch, scratch, var, ALU.mult))
    chain.link(dve.tensor_scalar(scratch, scratch, -0.5, 1.5, ALU.mult, ALU.add))
    chain.link(dve.tensor_tensor(rstd, rstd, scratch, ALU.mult))


def moe_phase(nc, tag, x_sb, K, xs, ys, W, E, shared):
    NJ = slot_tiles(E)
    with ExitStack() as ctx:
        def sb(name, shape, dt=F32):
            return ctx.enter_context(nc.sbuf_tensor(f"{tag}_{name}", shape, dt))

        def ps(name, shape, dt=F32):
            return ctx.enter_context(nc.psum_tensor(f"{tag}_{name}", shape, dt))

        def sem(name):
            return nc.alloc_semaphore(f"{tag}_{name}")

        wgu = sb("wgu", [P, KD, E, 2 * F])
        wdn = sb("wdn", [P, E, D])
        wr = sb("wr", [P, KD, E])
        bgu = bdn = ebias = wsgu = wsdn = xT_all = hs = None
        if shared:
            ebias = sb("ebias", [P, E])
            wsgu = sb("wsgu", [P, KD, 2 * SHARED])
            wsdn = sb("wsdn", [P, SHARED // P, D])
            xT_all = sb("xT_all", [P, KD, T])
            hs = sb("hs", [P, SHARED // P, SEQ])
            ssil = sb("ssil", [P, 2, SEQ])
        else:
            bgu = sb("bgu", [P, E, 2 * F])
            bdn = sb("bdn", [P, E, D])
        routing_consts = sb("routing", [P, sum(ROUTING.values())])
        R, at = {}, 0
        for name, n in ROUTING.items():
            R[name] = routing_consts[:, at:at + n]
            at += n
        xn = sb("xn", [P, NT, D])
        xn_t = [sb(f"xn_t{b}", [P, D]) for b in range(2)]
        xT = [sb(f"xT{b}", [P, KD, P]) for b in range(2)]
        stats = sb("stats", [P, NT, 6])
        mean = sb("mean", [P, NT])
        var = sb("var", [P, NT])
        root = sb("root", [P, NT])
        rstd = sb("rstd", [P, NT])
        logit = sb("logit", [P, NT, E])
        work = sb("work", [P, NT, E])
        hot = [sb(f"hot{k}", [P, NT, E]) for k in range(2)]
        both = sb("both", [P, NT, E])
        best = [sb(f"best{k}", [P, NT]) for k in range(2)]
        first = sb("first", [P, NT])
        wexp = sb("wexp", [P, NT])
        wsum = sb("wsum", [P, NT])
        share = [sb(f"share{k}", [P, NT]) for k in range(2)]
        count = sb("count", [P, E, NT])
        upto = sb("upto", [P, E, NT])
        tiles = sb("tiles", [P, E])
        tiles_upto = sb("tiles_upto", [P, E])
        base = sb("base", [P, E])
        placef = sb("placef", [P, NT])
        place = [sb(f"place{k}", [P, NT], I32) for k in range(2)]
        owner_cmp = sb("owner_cmp", [P, NJ, E])
        ownerf = sb("ownerf", [P, NJ])
        owner = sb("owner", [P, NJ], I32)
        x_in = [sb(f"x_in{b}", [P, D]) for b in range(2)]
        xsT = [sb(f"xsT{b}", [P, KD, P]) for b in range(2)]
        pre = [sb(f"pre{b}", [P, 2 * F]) for b in range(2)]
        gate = [sb(f"gate{b}", [P, F]) for b in range(2)]
        up = [sb(f"up{b}", [P, F]) for b in range(2)]
        sig = [sb(f"sig{b}", [P, F]) for b in range(2)]
        glu = [sb(f"glu{b}", [P, F]) for b in range(2)]
        hid = [sb(f"hid{b}", [P, F]) for b in range(2)]
        hidT = [sb(f"hidT{b}", [P, P]) for b in range(2)]
        y_out = [sb(f"y_out{b}", [P, D]) for b in range(2)]
        RING = 4
        y_got = [sb(f"y_got{r}", [P, 2, D]) for r in range(RING)]

        bank = [ps(f"bank{k}", [P, 512]) for k in range(8)]

        s_w = sem("weights_in")
        s_wr = sem("router_in")
        s_ch = sem("dve_chain")
        s_root = sem("root_ready")
        s_var = sem("var_ready")
        s_xn = sem("xn_ready")
        s_tr = sem("x_transposed")
        s_xt = sem("xT_ready")
        s_xta = sem("xT_all_ready")
        s_lg = sem("logits_done")
        s_both = sem("choices_ready")
        s_cnt = sem("counts_done")
        s_d = sem("margin_ready")
        s_we = sem("wexp_ready")
        s_place = sem("places_ready")
        s_scat = sem("rows_scattered")
        s_sgu = sem("shared_gu_done")
        s_ssil = sem("shared_silu_done")
        s_sh = sem("shared_hidden")
        s_sdn = sem("shared_down_done")
        s_sacc = sem("shared_added")

        NB = NT // TB

        routing = nc.Block()
        blk = routing.__enter__()

        @blk.sync
        def _(sp):
            sp.dma_start(wr[:], W["wr"]).then_inc(s_wr, 16)
            sp.dma_start(routing_consts[:], K["routing"]).then_inc(s_wr, 16)
            if shared:
                sp.dma_start(ebias[:], W["ebias"].partition_broadcast(P)).then_inc(s_wr, 16)
                sp.dma_start(wsgu[:], W["wsgu"]).then_inc(s_w, 16)
                sp.dma_start(wsdn[:], W["wsdn"]).then_inc(s_w, 16)
            else:
                sp.dma_start(bgu[:], W["bgu"].partition_broadcast(P)).then_inc(s_w, 16)
                sp.dma_start(bdn[:], W["bdn"].partition_broadcast(P)).then_inc(s_w, 16)
            sp.dma_start(wgu[:], W["wgu"]).then_inc(s_w, 16)
            sp.dma_start(wdn[:], W["wdn"]).then_inc(s_w, 16)
            sp.wait_ge(s_w, 64)
            sp.wait_ge(s_wr, 16 * (3 if shared else 2))

        @blk.gpsimd
        def _(pool):
            pool.wait_ge(s_place, 1)
            for i in range(NT):
                for k in range(2):
                    pool.indirect_dma_start(
                        xs[:, :], bass.IndirectOffsetOnAxis(ap=place[k][:, i:i + 1], axis=0),
                        xn[:, i, :], None).then_inc(s_scat, 16)
            pool.wait_ge(s_scat, 16 * 2 * NT)

        @blk.scalar
        def _(act):
            act.wait_ge(s_var, 1)
            act.activation(root[:], var[:], ACT.Sqrt).then_inc(s_root, 1)
            with act.Fori(0, NT - 1, 2) as i:
                for b in range(2):
                    act.wait_ge(s_tr, i + (b + 1))
                    act.wait_ge(s_lg, i)
                    act.activation(xT[b][:], bank[b][:, 0:D].rearrange("p (k t) -> p k t", k=KD),
                                   ACT.Copy).then_inc(s_xt, 1)
                    if shared:
                        act.activation(xT_all[:, :, ds(i * P + b * P, P)],
                                       bank[b][:, 0:D].rearrange("p (k t) -> p k t", k=KD),
                                       ACT.Copy).then_inc(s_xta, 1)
            act.wait_ge(s_d, 1)
            act.activation(wexp[:], wexp[:], ACT.Exp).then_inc(s_we, 1)
            if shared:
                with act.Fori(0, NB * 2 - 1, 2) as q:
                    for f in range(2):
                        act.wait_ge(s_sgu, q + (f + 1))
                        act.wait_ge(s_sh, q)
                        act.activation(ssil[:, f, :], bank[4 + f][:], ACT.Silu).then_inc(s_ssil, 1)

        @blk.tensor
        def _(pe):
            pe.wait_ge(s_wr, 16 * (3 if shared else 2))
            with pe.Fori(0, NT - 1, 2) as i:
                for b in range(2):
                    pe.wait_ge(s_xn, i + (b + 1))
                    pe.wait_ge(s_xt, i)
                    if shared:
                        pe.wait_ge(s_xta, i)
                    for k in range(KD):
                        mm = pe.transpose(bank[b][:, k * P:(k + 1) * P], xn_t[b][:, k * P:(k + 1) * P],
                                          K["ident"])
                    mm.then_inc(s_tr, 1)
                for b in range(2):
                    pe.wait_ge(s_xt, i + (b + 1))
                    for k in range(KD):
                        mm = pe.matmul(bank[2][:, ds(i * E + b * E, E)], xT[b][:, k, :], wr[:, k, :],
                                       start=(k == 0), stop=(k == KD - 1))
                    mm.then_inc(s_lg, 1)
            pe.wait_ge(s_both, 1)
            if shared:
                pe.wait_ge(s_xta, NT)
            pe.matmul(bank[0][:, 0:NT * E], R["before"], both[:].rearrange("p i e -> p (i e)"),
                      start=True, stop=True)
            pe.matmul(bank[1][:, 0:NT * E], R["ones"], both[:].rearrange("p i e -> p (i e)"),
                      start=True, stop=True).then_inc(s_cnt, 1)
            if shared:
                pe.wait_ge(s_w, 64)

                def gate_up(blk_i, f):
                    for half in range(2):
                        for k in range(KD):
                            mm = pe.matmul(bank[4 + 2 * half + f][:],
                                           wsgu[:, k, half * SHARED + f * P:half * SHARED + (f + 1) * P],
                                           xT_all[:, k, ds(blk_i * SEQ, SEQ)],
                                           start=(k == 0), stop=(k == KD - 1))
                    mm.then_inc(s_sgu, 1)

                with pe.Fori(0, NB, 1) as n:
                    for f in range(2):
                        pe.wait_ge(s_sh, n * 2)
                        gate_up(n, f)
                    pe.wait_ge(s_sh, n * 2 + 2)
                    for m in range(TB):
                        pe.wait_ge(s_sacc, n * TB + max(m - 1, 0))
                        for f in range(2):
                            mm = pe.matmul(bank[2 + m % 2][:, 0:D],
                                           hs[:, f, m * P:(m + 1) * P], wsdn[:, f, :],
                                           start=(f == 0), stop=(f == 1))
                        mm.then_inc(s_sdn, 1)

        @blk.vector
        def _(dve):
            c = Chain(dve, s_ch)
            layer_norm_stats(nc, dve, c, x_sb, stats, mean[:], var[:])
            dve.sem_inc(s_var, 1)
            dve.wait_ge(s_root, 1)
            layer_norm_rstd(dve, c, var[:], root[:], rstd[:], stats[:, :, 0])
            with dve.Fori(0, NT - 1, 2) as i:
                for b in range(2):
                    dve.wait_ge(s_tr, i)
                    dve.wait_ge(c.sem, c.n + i)
                    dve.tensor_scalar(xn_t[b][:], x_sb[:, ds(i + b, 1), :].rearrange("p a d -> p (a d)"),
                                      mean[:, ds(i + b, 1)], rstd[:, ds(i + b, 1)],
                                      ALU.subtract, ALU.mult).then_inc(s_xn, 1)
                for b in range(2):
                    dve.wait_ge(s_xn, i + (b + 1))
                    dve.tensor_copy(xn[:, ds(i + b, 1), :].rearrange("p a d -> p (a d)"),
                                    xn_t[b][:]).then_inc(c.sem, 1)
            c.n = c.n + NT
            c.wait()
            dve.wait_ge(s_lg, NT)
            lg = bank[2][:, 0:NT * E].rearrange("p (i e) -> p i e", e=E)
            full = [P, NT, E]
            dve.wait_ge(s_wr, 16 * (3 if shared else 2))
            if shared:
                c.link(dve.tensor_tensor(logit[:], lg, bcast(ebias[:].unsqueeze(1), full), ALU.add))
            else:
                c.link(dve.tensor_copy(logit[:], lg))
            number = bcast(R["e_less"][:, 0:E].unsqueeze(1), full)
            for k in range(2):
                c.link(dve.tensor_reduce(best[k][:], logit[:], AX.X, ALU.max))
                c.link(dve.tensor_tensor(work[:], logit[:], bcast(best[k][:].unsqueeze(2), full), ALU.is_equal))
                c.link(dve.tensor_tensor(work[:], work[:], number, ALU.mult))
                c.link(dve.tensor_reduce(first[:], work[:], AX.X, ALU.min))
                c.link(dve.tensor_tensor(hot[k][:], number, bcast(first[:].unsqueeze(2), full), ALU.is_equal))
                if k == 0:
                    c.link(dve.scalar_tensor_tensor(out=logit[:], in0=hot[0][:], scalar=MASKED, in1=logit[:],
                                                    op0=ALU.mult, op1=ALU.add))
            dve.tensor_tensor(both[:], hot[0][:], hot[1][:], ALU.add).then_inc(s_both, 1)
            dve.tensor_tensor(wexp[:], best[1][:], best[0][:], ALU.subtract).then_inc(s_d, 1)
            dve.wait_ge(s_cnt, 1)
            c.link(dve.tensor_copy(count[:], bank[1][:, 0:NT * E].rearrange("p (i e) -> p e i", e=E)))
            c.link(dve.tensor_tensor_scan(upto[:].rearrange("p e i -> p (e i)"), R["restart"][:, 0:E * NT],
                                          count[:].rearrange("p e i -> p (e i)"), 0.0, ALU.mult, ALU.add))
            c.link(dve.tensor_tensor(work[:].rearrange("p i e -> p (i e)").rearrange("p (e i) -> p e i", e=E),
                                     bcast(upto[:, :, NT - 1:NT], [P, E, NT]),
                                     bcast(R["tile_start"].unsqueeze(1), [P, E, NT]), ALU.is_gt))
            c.link(dve.tensor_reduce(tiles[:], work[:].rearrange("p i e -> p (i e)").rearrange("p (e i) -> p e i", e=E),
                                     AX.X, ALU.add))
            c.link(dve.tensor_tensor_scan(tiles_upto[:], R["ones"][:, 0:E], tiles[:], 0.0, ALU.mult, ALU.add))
            c.link(dve.tensor_tensor(base[:], tiles_upto[:], tiles[:], ALU.subtract))
            c.link(dve.tensor_scalar(base[:], base[:], float(P), None, ALU.mult))
            c.link(dve.tensor_tensor(upto[:], upto[:], count[:], ALU.subtract))
            c.link(dve.tensor_tensor(upto[:], upto[:], bcast(base[:].unsqueeze(2), [P, E, NT]), ALU.add))
            c.link(dve.tensor_tensor(logit[:], bank[0][:, 0:NT * E].rearrange("p (i e) -> p i e", e=E),
                                     upto[:].rearrange("p e i -> p i e"), ALU.add))
            for k in range(2):
                c.link(dve.tensor_tensor(work[:], hot[k][:], logit[:], ALU.mult))
                c.link(dve.tensor_reduce(placef[:], work[:], AX.X, ALU.add))
                c.link(dve.tensor_copy(place[k][:], placef[:]))
            dve.sem_inc(s_place, 1)
            c.link(dve.tensor_tensor(owner_cmp[:], bcast(tiles_upto[:].unsqueeze(1), [P, NJ, E]),
                                     bcast(R["j"][:, 0:NJ].unsqueeze(2), [P, NJ, E]), ALU.is_le))
            c.link(dve.tensor_reduce(ownerf[:], owner_cmp[:], AX.X, ALU.add))
            c.link(dve.tensor_scalar(owner[:], ownerf[:], float(E - 1), None, ALU.min))
            dve.wait_ge(s_we, 1)
            c.link(dve.tensor_scalar(wsum[:], wexp[:], 1.0, None, ALU.add))
            c.link(dve.reciprocal(wsum[:], wsum[:]))
            c.link(dve.tensor_scalar(share[0][:], wsum[:], 0.5, None, ALU.mult))
            c.link(dve.tensor_tensor(share[1][:], share[0][:], wexp[:], ALU.mult))
            if shared:
                with dve.Fori(0, NB, 1) as n:
                    for f in range(2):
                        dve.wait_ge(s_ssil, n * 2 + (f + 1))
                        dve.wait_ge(s_sdn, n * TB)
                        dve.tensor_tensor(hs[:, f, :], ssil[:, f, :], bank[6 + f][:],
                                          ALU.mult).then_inc(s_sh, 1)
                    for m in range(TB):
                        dve.wait_ge(s_sdn, n * TB + (m + 1))
                        row = x_sb[:, ds(n * TB + m, 1), :].rearrange("p a d -> p (a d)")
                        dve.scalar_tensor_tensor(out=row, in0=bank[2 + m % 2][:, 0:D],
                                                 scalar=0.5, in1=row, op0=ALU.mult,
                                                 op1=ALU.add).then_inc(s_sacc, 1)

        routing.__exit__(None, None, None)

        s_in = [sem(f"x_in{b}") for b in range(2)]
        s_str = sem("xs_transposed")
        s_sxt = sem("xsT_ready")
        s_gu = sem("gate_up_done")
        s_pre = sem("pre_read")
        s_gate = sem("gate_ready")
        s_sig = sem("sigmoid_done")
        s_hid = sem("hidden_ready")
        s_glu = sem("glu_ready")
        s_upr = sem("up_ready")
        s_htr = sem("hidden_transposed")
        s_hT = sem("hidT_ready")
        s_dn = sem("down_done")
        s_y = sem("y_ready")
        s_st = [sem(f"y_stored{b}") for b in range(2)]
        NH = NJ // 2
        GU, HT, DN = 1, 3, 4

        pX, pG, pH, pY = bank[0:2], bank[2:4], bank[4:6], bank[6:8]
        with nc.Block() as blk:
            @blk.sync
            def _(sp):
                with sp.Fori(0, NH, 1) as h:
                    for b in range(2):
                        sp.wait_ge(s_str, 2 * h)
                        sp.dma_start(x_in[b][:], xs[ds(h * (2 * P) + b * P, P), :]).then_inc(s_in[b], 16)

            @blk.gpsimd
            def _(pool):
                with pool.Fori(0, NH, 1) as h:
                    for b in range(2):
                        pool.wait_ge(s_y, 2 * h + (b + 1))
                        pool.dma_start(ys[ds(h * (2 * P) + b * P, P), :], y_out[b][:]).then_inc(s_st[b], 16)
                for b in range(2):
                    pool.wait_ge(s_st[b], 16 * NH)

            @blk.tensor
            def _(pe):
                def body(s, b):
                    if within(s, 0, NJ):
                        if isinstance(s, int):
                            pe.wait_ge(s_in[b], 16 * (s // 2 + 1))
                        else:
                            pe.wait_ge(s_in[b], (s - b) * 8 + 16)
                        if after(s, 2):
                            pe.wait_ge(s_sxt, s - 1)
                        for k in range(KD):
                            mm = pe.transpose(pX[b][:, k * P:(k + 1) * P], x_in[b][:, k * P:(k + 1) * P],
                                              K["ident"])
                        mm.then_inc(s_str, 1)
                    if within(s, GU, NJ):
                        j, c = s - GU, (b + GU) % 2
                        e = pe.value_load(owner[0:1, ds(j, 1)], min_val=0, max_val=E - 1)
                        pe.wait_ge(s_sxt, j + 1)
                        if after(j, 2):
                            pe.wait_ge(s_hid if shared else s_pre, j - 1)
                        for k in range(KD):
                            mm = pe.matmul(pG[c][:, 0:2 * F], xsT[c][:, k, :],
                                           wgu[:, k, ds(e, 1), :].rearrange("p a n -> p (a n)"),
                                           start=(k == 0), stop=(k == KD - 1))
                        mm.then_inc(s_gu, 1)
                    if within(s, HT, NJ):
                        j, c = s - HT, (b + HT) % 2
                        pe.wait_ge(s_hid, j + 1)
                        if after(j, 2):
                            pe.wait_ge(s_hT, j - 1)
                        pe.transpose(pH[c][:, 0:P], hid[c][:], K["ident"]).then_inc(s_htr, 1)
                    if within(s, DN, NJ):
                        j, c = s - DN, (b + DN) % 2
                        e = pe.value_load(owner[0:1, ds(j, 1)], min_val=0, max_val=E - 1)
                        pe.wait_ge(s_hT, j + 1)
                        if after(j, 2):
                            pe.wait_ge(s_y, j - 1)
                        pe.matmul(pY[c][:, 0:D], hidT[c][:], wdn[:, ds(e, 1), :].rearrange("p a n -> p (a n)"),
                                  start=True, stop=True).then_inc(s_dn, 1)

                steps(pe, NJ, DN, body)

            @blk.scalar
            def _(act):
                ST, HL = 1, 3

                def body(s, b):
                    if within(s, 0, NJ):
                        act.wait_ge(s_str, s + 1)
                        if after(s, 2):
                            act.wait_ge(s_gu, s - 1)
                        act.activation(xsT[b][:], pX[b][:, 0:D].rearrange("p (k t) -> p k t", k=KD),
                                       ACT.Copy).then_inc(s_sxt, 1)
                    if within(s, ST, NJ):
                        j, c = s - ST, (b + ST) % 2
                        if shared:
                            act.wait_ge(s_gu, j + 1)
                            if after(j, 2):
                                act.wait_ge(s_hid, j - 1)
                            act.activation(sig[c][:], pG[c][:, 0:F], ACT.Silu).then_inc(s_sig, 1)
                        else:
                            act.wait_ge(s_gate, j + 1)
                            if after(j, 2):
                                act.wait_ge(s_glu, j - 1)
                            act.activation(sig[c][:], gate[c][:], ACT.Sigmoid, scale=ALPHA).then_inc(s_sig, 1)
                    if within(s, HL, NJ):
                        j, c = s - HL, (b + HL) % 2
                        act.wait_ge(s_htr, j + 1)
                        if after(j, 2):
                            act.wait_ge(s_dn, j - 1)
                        act.activation(hidT[c][:], pH[c][:, 0:P], ACT.Copy).then_inc(s_hT, 1)

                steps(act, NJ, HL, body)

            @blk.vector
            def _(dve):
                def hidden(s, b):
                    if within(s, 1, NJ):
                        j, c = s - 1, (b + 1) % 2
                        e = dve.value_load(owner[0:1, ds(j, 1)], min_val=0, max_val=E - 1)
                        dve.wait_ge(s_gu, j + 1)
                        dve.tensor_tensor(pre[c][:], pG[c][:, 0:2 * F],
                                          bgu[:, ds(e, 1), :].rearrange("p a n -> p (a n)"),
                                          ALU.add).then_inc(s_pre, 1)
                        dve.wait_ge(s_pre, j + 1)
                        if after(j, 2):
                            dve.wait_ge(s_glu, j - 1)
                            dve.wait_ge(s_hid, j - 1)
                        dve.tensor_scalar(gate[c][:], pre[c][:, 0:F], LIMIT, None, ALU.min).then_inc(s_gate, 1)
                        dve.tensor_scalar(up[c][:], pre[c][:, F:2 * F], LIMIT, -LIMIT, ALU.min,
                                          ALU.max).then_inc(s_upr, 1)
                    if within(s, 2, NJ):
                        j, c = s - 2, (b + 2) % 2
                        dve.wait_ge(s_sig, j + 1)
                        dve.wait_ge(s_gate, j + 1)
                        dve.tensor_tensor(glu[c][:], gate[c][:], sig[c][:], ALU.mult).then_inc(s_glu, 1)
                        dve.wait_ge(s_glu, j + 1)
                        dve.wait_ge(s_upr, j + 1)
                        if after(j, 2):
                            dve.wait_ge(s_htr, j - 1)
                        dve.scalar_tensor_tensor(out=hid[c][:], in0=up[c][:], scalar=1.0, in1=glu[c][:],
                                                 op0=ALU.add, op1=ALU.mult).then_inc(s_hid, 1)

                def hidden_shared(s, b):
                    if within(s, 2, NJ):
                        j, c = s - 2, (b + 2) % 2
                        dve.wait_ge(s_sig, j + 1)
                        if after(j, 2):
                            dve.wait_ge(s_htr, j - 1)
                        dve.tensor_tensor(hid[c][:], sig[c][:], pG[c][:, F:2 * F],
                                          ALU.mult).then_inc(s_hid, 1)

                def body(s, b):
                    (hidden_shared if shared else hidden)(s, b)
                    if within(s, 4, NJ):
                        j, c = s - 4, (b + 4) % 2
                        if not shared:
                            e = dve.value_load(owner[0:1, ds(j, 1)], min_val=0, max_val=E - 1)
                        dve.wait_ge(s_dn, j + 1)
                        if isinstance(j, int):
                            if j >= 2:
                                dve.wait_ge(s_st[c], 16 * (j // 2))
                        else:
                            dve.wait_ge(s_st[c], (j - c) * 8)
                        if shared:
                            dve.tensor_copy(y_out[c][:], pY[c][:, 0:D]).then_inc(s_y, 1)
                        else:
                            dve.tensor_tensor(y_out[c][:], pY[c][:, 0:D],
                                              bdn[:, ds(e, 1), :].rearrange("p a n -> p (a n)"),
                                              ALU.add).then_inc(s_y, 1)

                steps(dve, NJ, 4, body)

        s_got = [sem(f"y_got{r}") for r in range(RING)]
        s_half = sem("first_added")
        s_used = sem("second_added")
        with nc.Block() as blk:
            @blk.gpsimd
            def _(pool):
                for i in range(NT):
                    if i >= RING:
                        pool.wait_ge(s_used, i - RING + 1)
                    for k in range(2):
                        pool.indirect_dma_start(
                            y_got[i % RING][:, k, :], None, ys[0:NJ * P, :],
                            bass.IndirectOffsetOnAxis(ap=place[k][:, i:i + 1], axis=0)
                        ).then_inc(s_got[i % RING], 16)

            @blk.vector
            def _(dve):
                with dve.Fori(0, NT // RING, 1) as q:
                    for r in range(RING):
                        row = x_sb[:, ds(q * RING + r, 1), :].rearrange("p a d -> p (a d)")
                        dve.wait_ge(s_got[r], q * 32 + 32)
                        for k in range(2):
                            if k == 1:
                                dve.wait_ge(s_half, q * RING + (r + 1))
                            dve.scalar_tensor_tensor(
                                out=row, in0=y_got[r][:, k, :], scalar=share[k][:, ds(q * RING + r, 1)],
                                in1=row, op0=ALU.mult, op1=ALU.add).then_inc(s_used if k else s_half, 1)


CH = 512
CB = CH // P
NS = 16
RANK = 64
TAPS = 4
LOG1P = (0.999999806, -0.499974054, 0.3327548, -0.24495463, 0.177452402, -0.107681677, 0.0440895953,
         -0.00853919577)


def batch_row_loop(eng, step):
    HEAD = 3
    for n in range(HEAD):
        step(0, 0, n, False, True, True)
    with eng.Fori(0, BATCH // 2 - 1, 1) as q:
        for par in range(2):
            for n in range(HEAD, NS):
                step(2 * q + par, par, n, True, True, True)
            for n in range(HEAD):
                step(2 * q + (par + 1), 1 - par, n, True, True, True)
    for b in (BATCH - 2, BATCH - 1):
        for n in range(HEAD, NS):
            step(b, b % 2, n, True, True, b < BATCH - 1)
        for n in range(HEAD):
            step(b + 1, 1 - b % 2, n, True, b < BATCH - 1, False)


def mamba_phase(nc, x_sb, K, A):
    with ExitStack() as ctx:
        def sb(name, shape, dt=F32):
            return ctx.enter_context(nc.sbuf_tensor(f"ssm_{name}", shape, dt))

        def sem(name):
            return nc.alloc_semaphore(f"ssm_{name}")

        win = sb("win", [P, KD, 2 * CH])
        wbd = sb("wbd", [P, KD, P])
        wdt = sb("wdt", [P, CH])
        wout = sb("wout", [P, CB, D])
        col = sb("col", [P, 3 * CB + 2 + CB * TAPS])
        bias_v, bias_x, bias_dt = (col[:, k * CB:(k + 1) * CB] for k in range(3))
        bias_bd = sb("bias_bd", [P, 1])
        tap = col[:, 3 * CB + 2:]
        decay = sb("decay", [P, CB, NS])
        cmat = sb("cmat", [P, CB, NS])
        cdiag = sb("cdiag", [P, NS, CB, P])
        bout = sb("bout", [P, D])
        mean, var, root, rstd = (sb(k, [P, NT]) for k in ("mean", "var", "root", "rstd"))
        xn_t = [sb(f"xn_t{k}", [P, D]) for k in range(2)]
        xnT = sb("xnT", [P, KD, SEQ])
        xpad = sb("xpad", [P, CB, TAPS - 1 + SEQ])
        sv = [sb(f"sv{k}", [P, CB, SEQ]) for k in range(2)]
        delta = [sb(f"delta{k}", [P, CB, SEQ]) for k in range(2)]
        dx = [sb(f"dx{k}", [P, CB, SEQ]) for k in range(2)]
        bd = [sb(f"bd{k}", [P, SEQ]) for k in range(2)]
        ex = sb("ex", [P, 2, SEQ])
        stats = ex[:, 0, 0:NT * 6].rearrange("p (i s) -> p i s", s=6)
        log = sb("log", [P, 2, SEQ])
        tmp = sb("tmp", [P, SEQ])
        dA = [sb(f"dA{k}", [P, CB, SEQ]) for k in range(2)]
        RH = 4
        hs = [sb(f"h{k}", [P, CB, SEQ]) for k in range(RH)]

        y_ps = ctx.enter_context(nc.psum_tensor("ssm_y_ps", [P, CB, SEQ], F32))
        b_ps = [ctx.enter_context(nc.psum_tensor(f"ssm_b_ps{k}", [P, SEQ], F32)) for k in range(2)]
        pj = [ctx.enter_context(nc.psum_tensor(f"ssm_pj{k}", [P, SEQ], F32)) for k in range(2)]

        s_w = sem("weights_in")
        s_chain = sem("dve_chain")
        s_var = sem("var_ready")
        s_root = sem("root_ready")
        s_dec = sem("decay_exp")
        s_neg = sem("decay_ready")
        s_set = sem("pads_ready")
        s_cd = sem("cdiag_ready")
        s_bias = sem("bias_ready")
        s_xn = sem("xn_ready")
        s_pj = sem("projected")
        s_ev = sem("evacuated_plus_1")
        s_conv = sem("convolved")
        s_silu = sem("silus_done")
        s_abs = sem("abs_done")
        s_ex = sem("ex_ready")
        s_poly = sem("log_steps")
        s_log = sem("log_ready")
        s_pool = sem("pool_chain")
        s_held = sem("held")
        s_delta = sem("delta_ready")
        s_dx = sem("dx_ready")
        s_xb = sem("bias_added")
        s_bb = sem("b_spread")
        s_da = sem("dA_ready")
        s_dbx = sem("dbx_ready_plus_16")
        s_scan = sem("scans_plus_1")
        s_diag = sem("summed_plus_3")
        s_g = sem("gated")
        s_op = sem("out_projected")
        s_xadd = sem("x_added")

        PIECES = ([("T", m, m // 2) for m in range(TB)] + [("X", c, 2 + c // 2) for c in range(CB)]
                  + [("BD", 0, 3)] + [("DT", 0, 4), ("DT", 1, 5)]
                  + [("V", c, 6 + c // 2) for c in range(CB)] + [("DT", 2, 9), ("DT", 3, 10)])
        USES = len(PIECES)
        USE = {(kind, k): u for u, (kind, k, _) in enumerate(PIECES)}
        POOL = [("conv", c) for c in range(CB)] + [("delta", c) for c in range(CB)] + [("dx", c) for c in range(CB)] + [("xb", m) for m in range(TB)]
        CHAIN = CB * (2 * TAPS - 2)
        LOG_STEPS = len(LOG1P)
        LOG_AT = (7, 12)
        SILU = 12

        def bank_of(f, fpar, u):
            return pj[(fpar * USES + u) % 2]

        with nc.Block() as blk:
            @blk.sync
            def _(sp):
                for dst, name in ((win, "win"), (wbd, "wbd"), (wdt, "wdt"), (wout, "wout"), (col, "col"),
                                  (decay, "alog"), (cmat, "cmat")):
                    sp.dma_start(dst[:], A["ssm_" + name]).then_inc(s_w, 16)
                sp.dma_start(bout[:], A["ssm_bout"].partition_broadcast(P)).then_inc(s_w, 16)
                sp.wait_ge(s_w, 128)

            @blk.gpsimd
            def _(pool):
                pool.wait_ge(s_w, 128)
                for n in range(NS):
                    for c in range(CB):
                        ins = pool.tensor_scalar(cdiag[:, n, c, :], K["ident"], cmat[:, c, n:n + 1], 0.0,
                                                 ALU.mult, ALU.add)
                ins.then_inc(s_cd, 1)


                def conv(f, fpar, c, k0):
                    pool.wait_ge(s_ev, f * USES + USE["X", c] + 2)
                    if c == 0:
                        pool.wait_ge(s_dbx, f * NS)
                    acc = dx[fpar][:, c, :]
                    for k in range(TAPS):
                        src = xpad[:, c, k:k + SEQ]
                        n = k0 + 2 * k
                        if k == 0:
                            pool.sem_inc(s_held, 1)
                        if k == 0:
                            pool.tensor_scalar(acc, src, tap[:, c * TAPS:c * TAPS + 1], 0.0,
                                               ALU.mult, ALU.add).then_inc(s_pool, 1)
                            continue
                        pool.sem_inc(s_held, 1)
                        pool.tensor_scalar(tmp[:], src, tap[:, c * TAPS + k:c * TAPS + k + 1], 0.0,
                                           ALU.mult, ALU.add).then_inc(s_pool, 1)
                        pool.wait_ge(s_pool, f * CHAIN + n)
                        ins = pool.tensor_tensor(acc, acc, tmp[:], ALU.add)
                        ins.then_inc(s_conv if k == TAPS - 1 else s_pool, 1)
                        if k < TAPS - 1:
                            pool.wait_ge(s_pool, f * CHAIN + n + 1)
                        else:
                            pool.wait_ge(s_conv, f * CB + c + 1)

                def soft(f, fpar, c):
                    pool.wait_ge(s_log, f * 2 + c // 2 + 1)
                    pool.tensor_tensor(delta[fpar][:, c, :], delta[fpar][:, c, :], log[:, c % 2, :],
                                       ALU.add).then_inc(s_delta, 1)
                    pool.wait_ge(s_delta, f * CB + c + 1)

                def row(f, fpar):
                    k0 = 0
                    for kind, k in POOL:
                        if kind == "conv":
                            conv(f, fpar, k, k0)
                            k0 += 2 * TAPS - 2
                        elif kind == "delta":
                            soft(f, fpar, k)
                        elif kind == "dx":
                            pool.wait_ge(s_silu, f * 2 + 2)
                            pool.tensor_tensor(dx[fpar][:, k, :], dx[fpar][:, k, :], delta[fpar][:, k, :],
                                               ALU.mult).then_inc(s_dx, 1)
                        else:
                            pool.wait_ge(s_xn, f * TB + k + 1)
                            x_row = x_sb[:, ds(f * TB + k, 1), :].rearrange("p a d -> p (a d)")
                            pool.tensor_tensor(x_row, x_row, bout[:], ALU.add).then_inc(s_xb, 1)
                    assert k0 == CHAIN

                pool.wait_ge(s_set, 1)
                with pool.Fori(0, BATCH // 2, 1) as q:
                    for fpar in range(2):
                        row(2 * q + fpar, fpar)

            @blk.scalar
            def _(act):
                act.wait_ge(s_w, 128)
                act.wait_ge(s_var, 1)
                act.activation(root[:], var[:], ACT.Sqrt).then_inc(s_root, 1)
                act.activation(decay[:], decay[:], ACT.Exp).then_inc(s_dec, 1)
                act.activation(bias_bd[:], col[:, 3 * CB:3 * CB + 1], ACT.Identity,
                               bias=col[:, 3 * CB + 1:3 * CB + 2]).then_inc(s_bias, 1)
                act.wait_ge(s_neg, 1)
                act.wait_ge(s_set, 1)
                act.wait_ge(s_bias, 1)
                act.sem_inc(s_ev, 1)
                act.preload_act_table_set("natural_log_exp_and_others")

                def piece(f, fpar, u):
                    kind, k, _ = PIECES[u]
                    src = bank_of(f, fpar, u)
                    old = not (isinstance(f, int) and f < 2)
                    act.wait_ge(s_pj, f * USES + u + 1)
                    if kind == "T":
                        act.activation(xnT[:, :, k * P:(k + 1) * P],
                                       src[:, 0:D].rearrange("p (k t) -> p k t", k=KD),
                                       ACT.Copy).then_inc(s_ev, 1)
                    elif kind == "X":
                        act.wait_ge(s_conv, f * CB)
                        act.activation(xpad[:, k, TAPS - 1:], src[:], ACT.Identity,
                                       bias=bias_x[:, k:k + 1]).then_inc(s_ev, 1)
                    elif kind == "V":
                        if old and k == 0:
                            act.wait_ge(s_op, (f - 1) * TB)
                        act.activation(sv[fpar][:, k, :], src[:], ACT.Identity,
                                       bias=bias_v[:, k:k + 1]).then_inc(s_ev, 1)
                    elif kind == "BD":
                        if old:
                            act.wait_ge(s_bb, (f - 1) * NS)
                        act.activation(bd[fpar][:], src[:], ACT.Identity,
                                       bias=bias_bd[:]).then_inc(s_ev, 1)
                    else:
                        act.wait_ge(s_delta, f * CB + k - k % 2)
                        if old and k == 0:
                            act.wait_ge(s_da, (f - 1) * NS)
                            act.wait_ge(s_dx, (f - 1) * CB)
                        act.activation(ex[:, k % 2, :], src[:], ACT.Abs,
                                       bias=bias_dt[:, k:k + 1]).then_inc(s_abs, 1)
                        act.activation(delta[fpar][:, k, :], src[:], ACT.Relu,
                                       bias=bias_dt[:, k:k + 1]).then_inc(s_ev, 1)
                        act.wait_ge(s_abs, f * CB + k + 1)
                        act.activation(ex[:, k % 2, :], ex[:, k % 2, :], ACT.Exp,
                                       scale=-1.0).then_inc(s_ex, 1)

                def silus(f, fpar):
                    act.wait_ge(s_ev, f * USES + USE["V", CB - 1] + 2)
                    act.activation(sv[fpar][:], sv[fpar][:], ACT.Silu).then_inc(s_silu, 1)
                    act.wait_ge(s_conv, (f + 1) * CB)
                    act.activation(dx[fpar][:], dx[fpar][:], ACT.Silu).then_inc(s_silu, 1)
                    act.preload_act_table_set("natural_log_exp_and_others")

                for u in range(USES):
                    piece(0, 0, u)
                silus(0, 0)

                def step(b, par, n, prev, main, front):
                    if main:
                        if n == 0:
                            act.wait_ge(s_delta, (b + 1) * CB)
                        act.wait_ge(s_scan, b * NS + n)
                        for c in range(CB):
                            ins = act.activation(dA[n % 2][:, c, 1:], delta[par][:, c, 1:], ACT.Exp,
                                                 scale=decay[:, c, n:n + 1])
                        ins.then_inc(s_da, 1)
                    if front:
                        for u, (_, _, at) in enumerate(PIECES):
                            if at == n - 1 or (at == NS - 1 and n == NS - 1):
                                piece(b + 1, 1 - par, u)
                        if n == SILU:
                            silus(b + 1, 1 - par)

                batch_row_loop(act, step)

            @blk.tensor
            def _(pe):
                def piece(f, fpar, u):
                    kind, k, _ = PIECES[u]
                    dst = bank_of(f, fpar, u)
                    pe.wait_ge(s_ev, f * USES + u)
                    if kind == "T":
                        pe.wait_ge(s_xn, f * TB + k + 1)
                        for kd in range(KD):
                            mm = pe.transpose(dst[:, kd * P:(kd + 1) * P], xn_t[k % 2][:, kd * P:(kd + 1) * P],
                                              K["ident"])
                    elif kind == "DT":
                        pe.wait_ge(s_ev, f * USES + USE["BD", 0] + 2)
                        mm = pe.matmul(dst[:], wdt[RANK:P, k * P:(k + 1) * P], bd[fpar][RANK:P, :],
                                       start=True, stop=True)
                    else:
                        if kind == "X" and k == 0:
                            pe.wait_ge(s_ev, f * USES + TB + 1)
                        w = wbd if kind == "BD" else win
                        at = {"V": k * P, "X": CH + k * P, "BD": 0}[kind]
                        for kd in range(KD):
                            mm = pe.matmul(dst[:], w[:, kd, at:at + P], xnT[:, kd, :],
                                           start=(kd == 0), stop=(kd == KD - 1))
                    mm.then_inc(s_pj, 1)

                def spread(b, par, n):
                    if n == 0:
                        pe.wait_ge(s_ev, b * USES + USE["BD", 0] + 2)
                    pe.wait_ge(s_dbx, b * NS + NS + max(n - 1, 0))
                    pe.matmul(b_ps[n % 2][:], K["ident"][0:NS, n:n + 1].broadcast_to([NS, P]),
                              bd[par][0:NS, :], start=True, stop=True).then_inc(s_bb, 1)

                def sums(b, par, n):
                    if n == 0:
                        pe.wait_ge(s_xadd, b * TB)
                    pe.wait_ge(s_scan, b * NS + n + 2)
                    for c in range(CB):
                        mm = pe.matmul(y_ps[:, c, :], cdiag[:, n, c, :], hs[n % RH][:, c, :],
                                       start=(n == 0), stop=(n == NS - 1))
                    mm.then_inc(s_diag, 1)

                def project(b, par):
                    pe.wait_ge(s_g, b + 1)
                    for m in range(TB):
                        for c in range(CB):
                            mm = pe.matmul(y_ps[:, m, 0:D], sv[par][:, c, m * P:(m + 1) * P], wout[:, c, :],
                                           start=(c == 0), stop=(c == CB - 1))
                        mm.then_inc(s_op, 1)

                pe.wait_ge(s_w, 128)
                pe.wait_ge(s_cd, 1)
                for u in range(USES):
                    piece(0, 0, u)
                spread(0, 0, 0)

                def step(b, par, n, prev, main, front):
                    if main and n < NS - 1:
                        spread(b, par, n + 1)
                    if n == 0:
                        if prev:
                            sums(b - 1, 1 - par, NS - 1)
                    else:
                        if n == 1 and prev:
                            project(b - 1, 1 - par)
                        if main:
                            sums(b, par, n - 1)
                    if front:
                        for u, (_, _, at) in enumerate(PIECES):
                            if at == n:
                                piece(b + 1, 1 - par, u)
                        if n == NS - 1:
                            spread(b + 1, 1 - par, 0)

                batch_row_loop(pe, step)

            @blk.vector
            def _(dve):
                c = Chain(dve, s_chain)
                for k in range(2):
                    dve.memset(dA[k][:, :, 0:1], 0.0).then_inc(c.sem, 1)
                dve.memset(xpad[:, :, 0:TAPS - 1], 0.0).then_inc(c.sem, 1)
                c.n = 3
                layer_norm_stats(nc, dve, c, x_sb, stats, mean[:], var[:])
                dve.sem_inc(s_set, 1)
                dve.sem_inc(s_var, 1)
                dve.sem_inc(s_scan, 1)
                dve.sem_inc(s_dbx, NS)
                dve.sem_inc(s_diag, 3)
                dve.wait_ge(s_dec, 1)
                dve.tensor_scalar(decay[:], decay[:], -1.0, None, ALU.mult).then_inc(s_neg, 1)
                dve.wait_ge(s_root, 1)
                layer_norm_rstd(dve, c, var[:], root[:], rstd[:], stats[:, :, 0])

                def norm(f, m):
                    dve.wait_ge(s_pj, f * USES + max(m - 1, 0))
                    dve.tensor_scalar(xn_t[m % 2][:],
                                      x_sb[:, ds(f * TB + m, 1), :].rearrange("p a d -> p (a d)"),
                                      mean[:, ds(f * TB + m, 1)], rstd[:, ds(f * TB + m, 1)],
                                      ALU.subtract, ALU.mult).then_inc(s_xn, 1)

                def dbx(b, par, n):
                    if n == 0:
                        dve.wait_ge(s_dx, (b + 1) * CB)
                    dve.wait_ge(s_bb, b * NS + n + 1)
                    dve.wait_ge(s_diag, b * NS + n)
                    dve.tensor_tensor(hs[n % RH][:], dx[par][:],
                                      b_ps[n % 2][:].unsqueeze(1).broadcast_to([P, CB, SEQ]),
                                      ALU.mult).then_inc(s_dbx, 1)

                def scan(b, n):
                    dve.wait_ge(s_da, b * NS + n + 1)
                    dve.wait_ge(s_dbx, b * NS + NS + n + 1)
                    h = hs[n % RH][:].rearrange("p c t -> p (c t)")
                    dve.tensor_tensor_scan(h, dA[n % 2][:].rearrange("p c t -> p (c t)"), h, 0.0,
                                           ALU.mult, ALU.add).then_inc(s_scan, 1)

                def log1p(f, g, k):
                    if k == 0:
                        dve.wait_ge(s_ex, f * CB + 2 * g + 2)
                        dve.wait_ge(s_delta, f * CB + 2 * g)
                        ins = dve.tensor_scalar(log[:], ex[:], LOG1P[-1], LOG1P[-2], ALU.mult, ALU.add)
                    else:
                        dve.wait_ge(s_poly, f * (2 * LOG_STEPS) + g * LOG_STEPS + k)
                        if k == 1:
                            ins = dve.tensor_tensor(log[:], log[:], ex[:], ALU.mult)
                        else:
                            ins = dve.scalar_tensor_tensor(out=log[:], in0=log[:], scalar=LOG1P[-1 - k], in1=ex[:],
                                                           op0=ALU.add, op1=ALU.mult)
                    ins.then_inc(s_poly, 1)
                    if k == LOG_STEPS - 1:
                        dve.wait_ge(s_poly, f * (2 * LOG_STEPS) + (g + 1) * LOG_STEPS)
                        dve.sem_inc(s_log, 1)

                def gated(b, par):
                    dve.wait_ge(s_diag, b * NS + NS + 3)
                    dve.wait_ge(s_silu, b * 2 + 1)
                    dve.tensor_tensor(sv[par][:], sv[par][:], y_ps[:], ALU.mult).then_inc(s_g, 1)

                def added(b):
                    for m in range(TB):
                        dve.wait_ge(s_op, b * TB + m + 1)
                        dve.wait_ge(s_xb, b * TB + m + 1)
                        x_row = x_sb[:, ds(b * TB + m, 1), :].rearrange("p a d -> p (a d)")
                        dve.tensor_tensor(x_row, x_row, y_ps[:, m, 0:D], ALU.add).then_inc(s_xadd, 1)

                for m in range(TB):
                    norm(0, m)
                for g in range(2):
                    for k in range(LOG_STEPS):
                        log1p(0, g, k)

                def step(b, par, n, prev, main, front):
                    if main:
                        dbx(b, par, n)
                    if n == 0:
                        if prev:
                            scan(b - 1, NS - 1)
                    elif main:
                        scan(b, n - 1)
                    if prev and n == 1:
                        gated(b - 1, 1 - par)
                    if prev and n == 2:
                        added(b - 1)
                    if front:
                        for kind, k, at in PIECES:
                            if kind == "T" and at == n:
                                norm(b + 1, k)
                        for g, start in enumerate(LOG_AT):
                            for k in range(LOG_STEPS):
                                if n == start + k // 3:
                                    log1p(b + 1, g, k)

                batch_row_loop(dve, step)


HEADS, HD = 16, 16
GROUP = 4
GROUPS = HEADS // GROUP
HP = P // GROUP


def attention_phase(nc, x_sb, K, A):
    with ExitStack() as ctx:
        def sb(name, shape, dt=F32):
            return ctx.enter_context(nc.sbuf_tensor(f"att_{name}", shape, dt))

        def ps(name, shape, dt=F32):
            return ctx.enter_context(nc.psum_tensor(f"att_{name}", shape, dt))

        def sem(name):
            return nc.alloc_semaphore(f"att_{name}")

        wq, wk = (sb(k, [P, KD, GROUPS * P]) for k in ("wq", "wk"))
        wv = sb("wv", [P, KD, D])
        wo = sb("wo", [P, GROUPS, D])
        q_bias, k_bias = (sb(k, [P, GROUPS, SEQ]) for k in ("q_bias", "k_bias"))
        maskf = sb("maskf", [P, P])
        mask, identb = sb("mask", [P, P], BF16), sb("identb", [P, P], BF16)
        stats = sb("stats", [P, NT, 6])
        mean, var, root, rstd = (sb(k, [P, NT]) for k in ("mean", "var", "root", "rstd"))
        xn_t = [sb(f"xn_t{k}", [P, D]) for k in range(2)]
        xnT = sb("xnT", [P, KD, SEQ])
        qT = [sb(f"qT{k}", [P, SEQ]) for k in range(2)]
        kT = [sb(f"kT{k}", [P, SEQ]) for k in range(2)]
        v = [sb(f"v{k}", [P, TB, GROUP, HP]) for k in range(2)]
        prob = [sb(f"prob{k}", [P, GROUP, SEQ]) for k in range(2)]
        top = [sb(f"top{k}", [P, GROUP]) for k in range(2)]
        total = [sb(f"total{k}", [P, GROUP]) for k in range(2)]
        inv = sb("inv", [P, GROUP])
        inv_b = sb("inv_b", [P, GROUP, HP])
        inv_t = sb("inv_t", [P, P])
        probT = [sb(f"probT{k}", [P, GROUP, P]) for k in range(2)]
        oT = sb("oT", [P, GROUPS, SEQ])

        sc = [ps(f"sc{j}", [P, SEQ]) for j in range(GROUP)]
        turn = [ps(f"turn{k}", [P, SEQ]) for k in range(2)]
        o_ps = ps("o_ps", [P, P])
        misc = ps("misc", [P, SEQ])

        s_w = sem("weights_in")
        s_chain = sem("dve_chain")
        s_var = sem("var_ready")
        s_root = sem("root_ready")
        s_c = sem("constants_ready")
        s_xn = sem("xn_ready")
        s_m = sem("misc_written")
        s_me = sem("misc_read")
        s_sc = sem("scores_ready")
        s_top = sem("top_ready")
        s_ex = sem("probs_ready")
        s_inv = sem("inv_ready")
        s_ib = sem("inv_b_ready")
        s_t = sem("turned")
        s_te = sem("turn_read_plus_1")
        s_pv = sem("pv_done_plus_1")
        s_at = sem("oT_ready")

        UNITS = GROUPS * TB

        def uses(has_next):
            out = []
            for u in range(UNITS):
                g, i = divmod(u, TB)
                if i < 3 and (g < GROUPS - 1 or has_next):
                    out.append((u, "QKV"[i], (g + 1) % GROUPS))
                if g == GROUPS - 2 and i == 3 and has_next:
                    out += [(u, "T", m) for m in range(TB)]
                if u == UNITS - 1:
                    out += [(u, "out", m) for m in range(TB)]
            return out

        FIRST = [(None, "T", m) for m in range(TB)] + [(None, k, 0) for k in "QKV"]
        M0, MU = len(FIRST), len(uses(True))
        TURNS = [sum(k + 2 for k in range(u % TB)) + u // TB * 14 for u in range(UNITS)]
        PVS = [sum(k + 1 for k in range(u % TB)) + u // TB * 10 for u in range(UNITS)]
        NTURN, NPV = 14 * GROUPS, 10 * GROUPS

        def rows_loop(eng, body):
            with eng.Fori(0, BATCH - 1, 1) as b:
                body(b, True)
            body(BATCH - 1, False)

        with nc.Block() as blk:
            @blk.sync
            def _(sp):
                for dst, name in ((wq, "wq"), (wk, "wk"), (wv, "wv"), (wo, "wo"), (q_bias, "q_bias"),
                                  (k_bias, "k_bias"), (maskf, "mask")):
                    sp.dma_start(dst[:], A["att_" + name]).then_inc(s_w, 16)
                sp.wait_ge(s_w, 112)

            @blk.scalar
            def _(act):
                act.wait_ge(s_var, 1)
                act.activation(root[:], var[:], ACT.Sqrt).then_inc(s_root, 1)
                act.wait_ge(s_w, 112)
                act.activation(mask[:], maskf[:], ACT.Copy).then_inc(s_c, 1)
                act.activation(identb[:], K["ident"], ACT.Copy).then_inc(s_c, 1)

                def tile_copy(at, m):
                    act.wait_ge(s_m, at + 1)
                    act.activation(xnT[:, :, m * P:(m + 1) * P],
                                   misc[:, 0:D].rearrange("p (k t) -> p k t", k=KD),
                                   ACT.Copy).then_inc(s_me, 1)

                def exps(b, u):
                    i = u % TB
                    for j in range(GROUP):
                        act.wait_ge(s_top, (b * UNITS + u) * GROUP + j + 1)
                        act.activation(prob[u % 2][:, j, 0:(i + 1) * P], sc[j][:, 0:(i + 1) * P], ACT.Exp,
                                       bias=top[u % 2][:, j:j + 1],
                                       accum_out=total[u % 2][:, j:j + 1]).then_inc(s_ex, 1)

                for n, (_, kind, m) in enumerate(FIRST):
                    if kind == "T":
                        tile_copy(n, m)
                act.preload_act_table_set("exp_and_others")
                exps(0, 0)

                def body(b, has_next):
                    for u in range(UNITS):
                        if u < UNITS - 1:
                            exps(b, u + 1)
                        elif has_next:
                            exps(b + 1, 0)
                        for n, (at, kind, m) in enumerate(uses(has_next)):
                            if at == u and kind == "T":
                                tile_copy(b * MU + M0 + n, m)

                rows_loop(act, body)

            @blk.tensor
            def _(pe):
                def use(at, kind, k):
                    pe.wait_ge(s_me, at)
                    if kind == "T":
                        pe.wait_ge(s_xn, tiles_before(at) + k + 1)
                        for kd in range(KD):
                            mm = pe.transpose(misc[:, kd * P:(kd + 1) * P],
                                              xn_t[k % 2][:, kd * P:(kd + 1) * P], K["ident"])
                    elif kind in "QK":
                        w = wq if kind == "Q" else wk
                        for kd in range(KD):
                            mm = pe.matmul(misc[:], w[:, kd, k * P:(k + 1) * P], xnT[:, kd, :],
                                           start=(kd == 0), stop=(kd == KD - 1))
                    elif kind == "V":
                        for m in range(TB):
                            for kd in range(KD):
                                mm = pe.matmul(misc[:, m * GROUP * HD:(m + 1) * GROUP * HD],
                                               xnT[:, kd, m * P:(m + 1) * P],
                                               wv[:, kd, k * GROUP * HD:(k + 1) * GROUP * HD],
                                               start=(kd == 0), stop=(kd == KD - 1))
                    else:
                        for g in range(GROUPS):
                            mm = pe.matmul(misc[:, 0:D], oT[:, g, k * P:(k + 1) * P], wo[:, g, :],
                                           start=(g == 0), stop=(g == GROUPS - 1))
                    mm.then_inc(s_m, 1)

                row = [0]

                def tiles_before(at):
                    return row[0]

                def scores(b, u, j, ready):
                    g, i = divmod(u, TB)
                    if ready is not None:
                        pe.wait_ge(s_ex, ready)
                    pe.matmul(sc[j][:, i * P:(i + 1) * P], identb[:], mask[:], start=True, stop=False,
                              skip_group_check=True)
                    rows = slice(j * HP, (j + 1) * HP)
                    pe.matmul(sc[j][:, 0:(i + 1) * P], qT[g % 2][rows, i * P:(i + 1) * P],
                              kT[g % 2][rows, 0:(i + 1) * P], start=False, stop=True,
                              skip_group_check=True).then_inc(s_sc, 1)

                def turn_pv(b, u):
                    g, i = divmod(u, TB)
                    pe.wait_ge(s_ex, (b * UNITS + u) * GROUP + GROUP)

                    def pv(kt):
                        n = b * NPV + PVS[u] + kt
                        pe.wait_ge(s_te, b * NTURN + TURNS[u] + kt + 2)
                        if kt == 0:
                            pe.wait_ge(s_at, b * UNITS + u)
                        for j in range(GROUP):
                            mm = pe.matmul(o_ps[j * HP:(j + 1) * HP, :], v[g % 2][:, kt, j, :],
                                           probT[(PVS[u] + kt) % 2][:, j, :], start=(kt == 0), stop=(kt == i))
                        mm.then_inc(s_pv, 1)

                    for kt in range(i + 1):
                        q = TURNS[u] + kt
                        pe.wait_ge(s_te, b * NTURN + q)
                        for j in range(GROUP):
                            mm = pe.transpose(turn[q % 2][:, j * P:(j + 1) * P],
                                              prob[u % 2][:, j, kt * P:(kt + 1) * P], K["ident"])
                        mm.then_inc(s_t, 1)
                        if kt > 0:
                            pv(kt - 1)
                    q = TURNS[u] + i + 1
                    pe.wait_ge(s_ib, b * UNITS + u + 1)
                    pe.wait_ge(s_te, b * NTURN + q)
                    pe.transpose(turn[q % 2][:, 0:P], inv_b[:].rearrange("p j r -> p (j r)"),
                                 K["ident"]).then_inc(s_t, 1)
                    pv(i)

                pe.wait_ge(s_w, 112)
                for n, (_, kind, k) in enumerate(FIRST):
                    use(n, kind, k)
                pe.wait_ge(s_c, 2)
                pe.wait_ge(s_me, M0)
                for j in range(GROUP):
                    scores(0, 0, j, None)

                def body(b, has_next):
                    row[0] = (b + 1) * TB
                    for u in range(UNITS):
                        nxt = u + 1
                        if nxt < UNITS or has_next:
                            if nxt % TB == 0:
                                done = [n for n, (at, _, _) in enumerate(uses(has_next)) if at <= u - 1]
                                pe.wait_ge(s_me, b * MU + M0 + done[-1] + 1)
                            for j in range(GROUP):
                                scores(b, nxt % UNITS, j, (b * UNITS + u) * GROUP + j + 1)
                        turn_pv(b, u)
                        for n, (at, kind, k) in enumerate(uses(has_next)):
                            if at == u:
                                if kind == "out" and k == 0:
                                    pe.wait_ge(s_at, (b + 1) * UNITS)
                                use(b * MU + M0 + n, kind, k)

                rows_loop(pe, body)

            @blk.vector
            def _(dve):
                c = Chain(dve, s_chain)
                for k in range(2):
                    c.step(dve.memset(v[k][:], 0.0))
                layer_norm_stats(nc, dve, c, x_sb, stats, mean[:], var[:])
                dve.sem_inc(s_var, 1)
                dve.sem_inc(s_te, 1)
                dve.sem_inc(s_pv, 1)
                dve.wait_ge(s_root, 1)
                layer_norm_rstd(dve, c, var[:], root[:], rstd[:], stats[:, :, 0])
                dve.wait_ge(s_w, 112)

                def norm(tile, m, at):
                    dve.wait_ge(s_m, at - 1 if m >= 2 else at - m)
                    dve.tensor_scalar(xn_t[m % 2][:],
                                      x_sb[:, ds(tile, 1), :].rearrange("p a d -> p (a d)"),
                                      mean[:, ds(tile, 1)], rstd[:, ds(tile, 1)],
                                      ALU.subtract, ALU.mult).then_inc(s_xn, 1)

                def read(at, kind, k, b):
                    if kind == "T":
                        return
                    dve.wait_ge(s_m, at + 1)
                    if kind == "Q":
                        dve.scalar_tensor_tensor(out=qT[k % 2][:], in0=misc[:], scalar=HD ** -0.5,
                                                 in1=q_bias[:, k, :], op0=ALU.mult, op1=ALU.add).then_inc(s_me, 1)
                    elif kind == "K":
                        dve.tensor_tensor(kT[k % 2][:], misc[:], k_bias[:, k, :], ALU.add).then_inc(s_me, 1)
                    elif kind == "V":
                        dve.tensor_copy(v[k % 2][:, :, :, 0:HD],
                                        misc[:, 0:TB * GROUP * HD].rearrange("p (m j d) -> p m j d", m=TB,
                                                                             j=GROUP)).then_inc(s_me, 1)
                    else:
                        x_row = x_sb[:, ds(b * TB + k, 1), :].rearrange("p a d -> p (a d)")
                        dve.tensor_tensor(x_row, x_row, misc[:, 0:D], ALU.add).then_inc(s_me, 1)

                def tops(b, u):
                    i = u % TB
                    for j in range(GROUP):
                        dve.wait_ge(s_sc, (b * UNITS + u) * GROUP + j + 1)
                        dve.tensor_reduce(top[u % 2][:, j:j + 1], sc[j][:, 0:(i + 1) * P], AX.X, ALU.max,
                                          negate=True).then_inc(s_top, 1)

                def inverse(b, u):
                    dve.wait_ge(s_ex, (b * UNITS + u) * GROUP + GROUP)
                    dve.reciprocal(inv[:], total[u % 2][:]).then_inc(s_inv, 1)
                    dve.wait_ge(s_inv, b * UNITS + u + 1)
                    dve.tensor_copy(inv_b[:], inv[:].unsqueeze(2).broadcast_to([P, GROUP, HP])).then_inc(s_ib, 1)

                def turned(b, u):
                    g, i = divmod(u, TB)
                    for kt in range(i + 1):
                        q = TURNS[u] + kt
                        dve.wait_ge(s_t, b * NTURN + q + 1)
                        dve.wait_ge(s_pv, b * NPV + PVS[u] + kt)
                        dve.tensor_copy(probT[(PVS[u] + kt) % 2][:].rearrange("p j t -> p (j t)"),
                                        turn[q % 2][:]).then_inc(s_te, 1)
                    q = TURNS[u] + i + 1
                    dve.wait_ge(s_t, b * NTURN + q + 1)
                    dve.tensor_copy(inv_t[:], turn[q % 2][:, 0:P]).then_inc(s_te, 1)
                    dve.wait_ge(s_te, b * NTURN + q + 2)
                    dve.wait_ge(s_pv, b * NPV + PVS[u] + i + 2)
                    if g == 0:
                        dve.wait_ge(s_m, b * MU + M0)
                    dve.tensor_tensor(oT[:, g, i * P:(i + 1) * P], o_ps[:], inv_t[:], ALU.mult).then_inc(s_at, 1)

                for n, (_, kind, k) in enumerate(FIRST):
                    if kind == "T":
                        norm(k, k, n)
                for n, (_, kind, k) in enumerate(FIRST):
                    read(n, kind, k, 0)
                tops(0, 0)

                def body(b, has_next):
                    for u in range(UNITS):
                        inverse(b, u)
                        if u < UNITS - 1:
                            tops(b, u + 1)
                        elif has_next:
                            tops(b + 1, 0)
                        turned(b, u)
                        for n, (at, kind, k) in enumerate(uses(has_next)):
                            if at == u and kind == "T":
                                norm((b + 1) * TB + k, k, b * MU + M0 + n)
                        for n, (at, kind, k) in enumerate(uses(has_next)):
                            if at == u:
                                read(b * MU + M0 + n, kind, k, b)

                rows_loop(dve, body)




def macaron_kernel(nc, A, out, phases=("moe0", "mamba", "moe0", "moe1", "attn", "moe1")):
    with ExitStack() as ctx:
        def sb(name, shape, dt=F32):
            return ctx.enter_context(nc.sbuf_tensor(name, shape, dt))

        x_sb = sb("x_sb", [P, NT, D])
        ident = sb("ident", [P, P])
        K = {"ident": ident[:], "routing": A["routing"]}
        xs = nc.dram_tensor("rows_by_slot", [slot_tiles(E0) * P, D], F32).ap()
        ys = nc.dram_tensor("results_by_slot", [slot_tiles(E0) * P, D], F32).ap()

        s_x = nc.alloc_semaphore("x_in")
        s_zero = nc.alloc_semaphore("zero_ready")
        s_clear = nc.alloc_semaphore("slots_cleared")
        s_out = nc.alloc_semaphore("x_stored")
        tokens = A["x"].rearrange("(i p) d -> p i d", p=P)

        with nc.sbuf_tensor("zero", [P, 1, D], F32) as zero:
            with nc.Block() as blk:
                @blk.sync
                def _(sp):
                    sp.dma_start(ident[:], A["ident"]).then_inc(s_x, 16)
                    sp.dma_start(x_sb[:], tokens).then_inc(s_x, 16)
                    sp.wait_ge(s_x, 32)

                @blk.vector
                def _(dve):
                    dve.memset(zero[:], 0.0).then_inc(s_zero, 1)

                @blk.scalar
                def _(act):
                    act.wait_ge(s_zero, 1)
                    act.dma_start(xs.rearrange("(p r) d -> p r d", p=P),
                                  zero[:].broadcast_to([P, slot_tiles(E0), D])).then_inc(s_clear, 16)
                    act.wait_ge(s_clear, 16)

        for n, phase in enumerate(phases):
            with nc.cleanup_on_exit():
                if phase == "moe0":
                    moe_phase(nc, f"f{n}", x_sb, K, xs, ys,
                              {k: A["m0_" + k] for k in ("wgu", "wdn", "wr", "bgu", "bdn")}, E0, False)
                elif phase == "moe1":
                    moe_phase(nc, f"f{n}", x_sb, K, xs, ys,
                              {k: A["m1_" + k] for k in ("wgu", "wdn", "wr", "ebias", "wsgu", "wsdn")}, E1, True)
                elif phase == "mamba":
                    mamba_phase(nc, x_sb, K, A)
                else:
                    attention_phase(nc, x_sb, K, A)

        with nc.Block() as blk:
            @blk.sync
            def _(sp):
                sp.dma_start(out.rearrange("(i p) d -> p i d", p=P), x_sb[:]).then_inc(s_out, 16)
                sp.wait_ge(s_out, 16)


def laid_out(np, inputs):
    g = {k: np.asarray(v) for k, v in inputs.items()}
    rows = lambda a: np.ascontiguousarray(
        a.reshape(a.shape[0] // P, P, a.shape[1]).transpose(1, 0, 2))
    A = {"x": g["L0_attn_input"].reshape(T, D)}
    gu = g["L0_ffn_gate_up_proj"]
    split = lambda a: np.concatenate([a[..., ::2], a[..., 1::2]], axis=-1)
    by_expert = lambda a: np.ascontiguousarray(
        a.reshape(a.shape[0], a.shape[1] // P, P, a.shape[2]).transpose(2, 1, 0, 3))
    A["m0_wgu"] = by_expert(split(gu))
    A["m0_wdn"] = by_expert(g["L0_ffn_down_proj"])[:, 0]
    A["m0_wr"] = rows(g["L0_ffn_router_weight"])
    A["m0_bgu"] = split(g["L0_ffn_gate_up_proj_bias"])
    A["m0_bdn"] = g["L0_ffn_down_proj_bias"]
    A["m1_wgu"] = by_expert(np.concatenate([g["L1_ffn_Wg"], g["L1_ffn_Wu"]], axis=-1))
    A["m1_wdn"] = by_expert(g["L1_ffn_Wd"])[:, 0]
    A["m1_wr"] = rows(g["L1_ffn_Wr"])
    A["m1_ebias"] = g["L1_ffn_expert_bias"]
    A["m1_wsgu"] = rows(np.concatenate([g["L1_ffn_Sg"], g["L1_ffn_Su"]], axis=-1))
    A["m1_wsdn"] = rows(g["L1_ffn_Sd"])
    win, b_in = g["L0_attn_Win"].T, g["L0_attn_b_in"]
    A["ssm_win"] = rows(np.ascontiguousarray(win[:, :2 * CH]))
    gap = lambda a: np.concatenate([a[..., :NS], np.zeros((*a.shape[:-1], RANK - NS), np.float32),
                                    a[..., NS:]], axis=-1)
    A["ssm_wbd"] = rows(gap(win[:, 2 * CH:]))
    A["ssm_wdt"] = np.concatenate([np.zeros((RANK, CH), np.float32), g["L0_attn_Wdt"].T])
    A["ssm_wout"] = rows(g["L0_attn_Wout"].T)
    blocks = lambda a: a.reshape(-1, P).T
    b_param = np.concatenate([g["L0_attn_B_param"], np.zeros(P - NS, np.float32)])
    A["ssm_col"] = np.concatenate(
        [blocks(b_in[:2 * CH]), blocks(g["L0_attn_b_dt"]), blocks(gap(b_in[2 * CH:])), blocks(b_param),
         g["L0_attn_Wconv"].reshape(CB, P, TAPS).transpose(1, 0, 2).reshape(P, CB * TAPS)], axis=1)
    A["ssm_alog"] = g["L0_attn_A_log"].reshape(CB, P, NS).transpose(1, 0, 2)
    A["ssm_cmat"] = g["L0_attn_C_param"].reshape(CB, P, NS).transpose(1, 0, 2)
    A["ssm_bout"] = g["L0_attn_b_out"]
    def spaced(a):
        out = np.zeros((a.shape[0], HEADS, HP), np.float32)
        out[:, :, :HD] = a.reshape(a.shape[0], HEADS, HD)
        return out.reshape(a.shape[0], HEADS * HP)
    A["att_wq"] = rows(spaced(g["L1_attn_W_Q"].T))
    A["att_wk"] = rows(spaced(g["L1_attn_W_K"].T))
    A["att_wv"] = rows(g["L1_attn_W_V"].T)
    A["att_wo"] = rows(np.ascontiguousarray(spaced(g["L1_attn_W_O"]).T))
    slope = (1.0 / (2.0 ** 8) ** ((np.arange(HEADS, dtype=np.float32) + 1) / HEADS)).astype(np.float32)
    place = (np.arange(SEQ) - SEQ // 2).astype(np.float32)
    q_bias, k_bias = (np.zeros((GROUPS, GROUP, HP, SEQ), np.float32) for _ in range(2))
    steep = slope.reshape(GROUPS, GROUP)[:, :, None] * place
    q_bias[:, :, HD], k_bias[:, :, HD] = 1.0, steep
    q_bias[:, :, HD + 1], k_bias[:, :, HD + 1] = -steep, 1.0
    for name, a in (("att_q_bias", q_bias), ("att_k_bias", k_bias)):
        A[name] = a.transpose(1, 2, 0, 3).reshape(P, GROUPS, SEQ)
    q = np.arange(P)
    A["att_mask"] = np.where(q[None, :] <= q[:, None], 0.0, MASKED).astype(np.float32)
    p = np.arange(P)
    consts = {
        "before": p[:, None] < p[None, :], "ones": np.ones((P, P)),
        "e_less": np.broadcast_to(np.arange(E0) - 64, (P, E0)),
        "restart": np.broadcast_to((np.arange(E0 * NT) % NT) > 0, (P, E0 * NT)),
        "tile_start": np.broadcast_to(np.arange(NT) * P, (P, NT)),
        "j": np.broadcast_to(np.arange(slot_tiles(E0)), (P, slot_tiles(E0))),
    }
    A["routing"] = np.concatenate([consts[k].astype(np.float32) for k in ROUTING], axis=1)
    A["ident"] = np.eye(P, dtype=np.float32)
    A = {k: np.ascontiguousarray(v) for k, v in A.items()}
    return A


def kernel(**inputs):
    import numpy as _np
    import concourse.bacc as _bacc
    from concourse import mybir as _mybir
    from concourse.bass_utils import run_bass_kernel_spmd as _run

    nc = _bacc.Bacc("TRN2", target_bir_lowering=False, num_devices=1)
    arrays = {f"in_{k}_dram": v for k, v in laid_out(_np, inputs).items()}
    args = {k[3:-5]: nc.dram_tensor(k, a.shape, _mybir.dt.from_np(a.dtype), kind="ExternalInput").ap()
            for k, a in arrays.items()}
    out = nc.dram_tensor("out_0_dram", (T, D), _mybir.dt.float32, kind="ExternalOutput").ap()
    macaron_kernel(nc, args, out)
    r = _run(nc, [arrays], core_ids=[0])
    return r.results[0]["out_0_dram"].reshape(BATCH, SEQ, D)
```

```python
from contextlib import ExitStack

import concourse.bass as bass
from concourse import mybir

ALU = mybir.AluOpType
ACT = mybir.ActivationFunctionType
AX = mybir.AxisListType
F32 = mybir.dt.float32
BF16 = mybir.dt.bfloat16
I32 = mybir.dt.int32
ds = bass.ds

P = 128
BATCH, SEQ, D = 8, 512, 256
T = BATCH * SEQ
NT = T // P
KD = D // P
TB = SEQ // P
EPS = 1e-5
MASKED = -1e30

F = 128
E0, E1 = 16, 8
SHARED = 256
LIMIT, ALPHA = 7.0, 1.702
UNROLL = 4


def slot_tiles(experts):
    most = (2 * T - experts) // P + experts
    return -(-most // UNROLL) * UNROLL


ROUTING = {"before": P, "ones": P, "e_less": E0, "restart": E0 * NT, "tile_start": NT,
           "j": slot_tiles(E0)}


class Chain:

    def __init__(self, eng, sem, n=0):
        self.eng, self.sem, self.n = eng, sem, n

    def step(self, ins):
        ins.then_inc(self.sem, 1)
        self.n = self.n + 1
        return self.n

    def wait(self):
        self.eng.wait_ge(self.sem, self.n)

    def link(self, ins):
        self.step(ins)
        self.wait()


def steps(eng, count, lead, lag, body):
    first = -(-(lag + UNROLL) // UNROLL) * UNROLL
    last = (count - lead) // UNROLL * UNROLL
    for s in range(-lead, first):
        body(s, s % UNROLL)
    with eng.Fori(first, last - UNROLL + 1, UNROLL) as i:
        for u in range(UNROLL):
            body(i + u, u)
    for s in range(last, count + lag):
        body(s, s % UNROLL)


def within(s, lag, count):
    return not isinstance(s, int) or 0 <= s - lag < count


def after(j, n):
    return not isinstance(j, int) or j >= n


def bcast(ap, shape):
    return ap.broadcast_to(shape)


def layer_norm_stats(dve, chain, x_sb, stats, mean, var, tiles=(0, NT)):
    with dve.Fori(tiles[0], tiles[1] - UNROLL + 1, UNROLL) as i:
        for u in range(UNROLL):
            dve.bn_stats(stats[:, ds(i + u, 1), :].rearrange("p a s -> p (a s)"),
                         x_sb[:, ds(i + u, 1), :].rearrange("p a d -> p (a d)")).then_inc(chain.sem, 1)
    chain.n = chain.n + tiles[1] - tiles[0]
    chain.wait()
    at = slice(*tiles)
    me, m2e, mo, m2o = (stats[:, at, k] for k in (1, 2, 4, 5))
    diff, square = stats[:, at, 0], stats[:, at, 3]
    chain.step(dve.tensor_tensor(mean[:, at], me, mo, ALU.add))
    chain.step(dve.tensor_tensor(var[:, at], m2e, m2o, ALU.add))
    chain.link(dve.tensor_tensor(diff, me, mo, ALU.subtract))
    chain.step(dve.tensor_scalar(mean[:, at], mean[:, at], 0.5, None, ALU.mult))
    chain.link(dve.tensor_tensor(square, diff, diff, ALU.mult))
    chain.link(dve.tensor_scalar(square, square, 0.25, EPS, ALU.mult, ALU.add))
    chain.link(dve.scalar_tensor_tensor(out=var[:, at], in0=var[:, at], scalar=1.0 / D, in1=square,
                                        op0=ALU.mult, op1=ALU.add))


def layer_norm_rstd(dve, chain, var, root, rstd, scratch, tiles=(0, NT)):
    at = slice(*tiles)
    var, root, rstd, scratch = var[:, at], root[:, at], rstd[:, at], scratch[:, at]
    chain.link(dve.reciprocal(rstd, root))
    chain.link(dve.tensor_tensor(scratch, rstd, rstd, ALU.mult))
    chain.link(dve.tensor_tensor(scratch, scratch, var, ALU.mult))
    chain.link(dve.tensor_scalar(scratch, scratch, -0.5, 1.5, ALU.mult, ALU.add))
    chain.link(dve.tensor_tensor(rstd, rstd, scratch, ALU.mult))


def moe_phase(nc, tag, x_sb, K, xs, ys, W, E, shared, clear=False, out=None):
    NJ = slot_tiles(E)
    with ExitStack() as ctx:
        def sb(name, shape, dt=F32):
            return ctx.enter_context(nc.sbuf_tensor(f"{tag}_{name}", shape, dt))

        def ps(name, shape, dt=F32):
            return ctx.enter_context(nc.psum_tensor(f"{tag}_{name}", shape, dt))

        def sem(name):
            return nc.alloc_semaphore(f"{tag}_{name}")

        wgu = sb("wgu", [P, KD, E, 2 * F])
        wdn = sb("wdn", [P, E, D])
        wr = sb("wr", [P, KD, E])
        bgu = bdn = ebias = wsgu = wsdn = xT_all = hs = None
        if shared:
            ebias = sb("ebias", [P, E])
            wsgu = sb("wsgu", [P, KD, 2 * SHARED])
            wsdn = sb("wsdn", [P, SHARED // P, D])
            xT_all = sb("xT_all", [P, KD, T])
            hs = sb("hs", [P, SHARED // P, SEQ])
            ssil = sb("ssil", [P, 2, SEQ])
        else:
            bgu = sb("bgu", [P, E, 2 * F])
            bdn = sb("bdn", [P, E, D])
        routing_consts = sb("routing", [P, sum(ROUTING.values())])
        R, at = {}, 0
        for name, n in ROUTING.items():
            R[name] = routing_consts[:, at:at + n]
            at += n
        xn = sb("xn", [P, NT, D])
        xn_t = [sb(f"xn_t{b}", [P, D]) for b in range(UNROLL)]
        RING = 4
        y_got = [sb(f"y_got{r}", [P, 2, D]) for r in range(RING)]
        xT = [y_got[b // 2][:, b % 2, :].rearrange("p (k t) -> p k t", k=KD) for b in range(2 * UNROLL)]
        stats = sb("stats", [P, NT, 6])
        mean = sb("mean", [P, NT])
        var = sb("var", [P, NT])
        root = sb("root", [P, NT])
        rstd = sb("rstd", [P, NT])
        logit = sb("logit", [P, NT, E])
        work = sb("work", [P, NT, E])
        hot = [sb(f"hot{k}", [P, NT, E]) for k in range(2)]
        both = sb("both", [P, NT, E])
        best = [sb(f"best{k}", [P, NT]) for k in range(2)]
        first = sb("first", [P, NT])
        wexp = sb("wexp", [P, NT])
        wsum = sb("wsum", [P, NT])
        share = [sb(f"share{k}", [P, NT]) for k in range(2)]
        count = sb("count", [P, E, NT])
        upto = sb("upto", [P, E, NT])
        tiles = sb("tiles", [P, E])
        tiles_upto = sb("tiles_upto", [P, E])
        base = sb("base", [P, E])
        placef = sb("placef", [P, NT])
        place = [sb(f"place{k}", [P, NT], I32) for k in range(2)]
        owner_cmp = sb("owner_cmp", [P, NJ, E])
        ownerf = sb("ownerf", [P, NJ])
        owner = sb("owner", [P, NJ], I32)
        x_in = [sb(f"x_in{b}", [P, D]) for b in range(UNROLL)]
        xsT = [sb(f"xsT{b}", [P, KD, P]) for b in range(2)]
        pre = [sb(f"pre{b}", [P, 2 * F]) for b in range(2)]
        gate = [sb(f"gate{b}", [P, F]) for b in range(2)]
        up = [sb(f"up{b}", [P, F]) for b in range(2)]
        sig = [sb(f"sig{b}", [P, F]) for b in range(2)]
        glu = [sb(f"glu{b}", [P, F]) for b in range(2)]
        hid = [sb(f"hid{b}", [P, F]) for b in range(2)]
        hidT = [sb(f"hidT{b}", [P, P]) for b in range(2)]
        y_out = [sb(f"y_out{q}", [P, 2, D]) for q in range(2)]

        bank = [ps(f"bank{k}", [P, 512]) for k in range(8)]

        s_w = sem("weights_in")
        s_wr = sem("router_in")
        s_ch = sem("dve_chain")
        s_root = sem("root_ready")
        s_var = sem("var_ready")
        s_xn = sem("xn_ready")
        s_tr = sem("x_transposed_plus_4")
        s_xt = sem("xT_ready_plus_4")
        s_cp = sem("xn_copied_plus_4")
        s_xta = sem("xT_all_ready_plus_4")
        s_lg = sem("logits_done_plus_8")
        s_both = sem("choices_ready")
        s_cnt = sem("counts_done")
        s_d = sem("margin_ready")
        s_we = sem("wexp_ready")
        s_place = sem("places_ready")
        s_zero = sem("zero_ready")
        s_clear = sem("slots_cleared")
        s_scat = sem("rows_scattered")
        s_sgu = sem("shared_gu_done")
        s_ssil = sem("shared_silu_done")
        s_sh = sem("shared_hidden_plus_2")
        s_sdn = sem("shared_down_done_plus_1")
        s_sacc = sem("shared_added_plus_2")

        NB = NT // TB
        CHUNK = 8

        pT = [bank[k] for k in (0, 1, 3, 4)]

        routing = nc.Block()
        blk = routing.__enter__()

        @blk.sync
        def _(sp):
            sp.dma_start(wr[:], W["wr"]).then_inc(s_wr, 16)
            sp.dma_start(routing_consts[:], K["routing"]).then_inc(s_wr, 16)
            if shared:
                sp.dma_start(ebias[:], W["ebias"].partition_broadcast(P)).then_inc(s_wr, 16)
                sp.dma_start(wsgu[:], W["wsgu"]).then_inc(s_w, 16)
                sp.dma_start(wsdn[:], W["wsdn"]).then_inc(s_w, 16)
            else:
                sp.dma_start(bgu[:], W["bgu"].partition_broadcast(P)).then_inc(s_w, 16)
                sp.dma_start(bdn[:], W["bdn"].partition_broadcast(P)).then_inc(s_w, 16)
            sp.dma_start(wgu[:], W["wgu"]).then_inc(s_w, 16)
            sp.dma_start(wdn[:], W["wdn"]).then_inc(s_w, 16)
            sp.wait_ge(s_w, 64)
            sp.wait_ge(s_wr, 16 * (3 if shared else 2))

        @blk.gpsimd
        def _(pool):
            if clear:
                pool.memset(x_in[0][:], 0.0).then_inc(s_zero, 1)
                pool.wait_ge(s_clear, 16)
            pool.wait_ge(s_place, 1)
            for i in range(NT):
                for k in range(2):
                    pool.indirect_dma_start(
                        xs[:, :], bass.IndirectOffsetOnAxis(ap=place[k][:, i:i + 1], axis=0),
                        xn[:, i, :], None).then_inc(s_scat, 16)
            pool.wait_ge(s_scat, 16 * 2 * NT)

        @blk.scalar
        def _(act):
            if clear:
                act.wait_ge(s_wr, 16 * (3 if shared else 2))
                act.wait_ge(s_zero, 1)
                act.dma_start(xs.rearrange("(p r) d -> p r d", p=P),
                              x_in[0][:].unsqueeze(1).broadcast_to([P, xs.shape[0] // P, D])).then_inc(s_clear, 16)

            def roots(k):
                act.wait_ge(s_var, k + 1)
                act.activation(root[:, k * CHUNK:(k + 1) * CHUNK], var[:, k * CHUNK:(k + 1) * CHUNK],
                               ACT.Sqrt).then_inc(s_root, 1)

            roots(0)
            act.sem_inc(s_xt, UNROLL)
            act.sem_inc(s_xta, UNROLL)
            for k in range(NT // CHUNK):
                if k < NT // CHUNK - 1:
                    roots(k + 1)
                with act.Fori(k * CHUNK, (k + 1) * CHUNK - 2 * UNROLL + 1, 2 * UNROLL) as i:
                    for v in range(2 * UNROLL):
                        u = v % UNROLL
                        act.wait_ge(s_tr, i + (v + 1 + UNROLL))
                        act.wait_ge(s_lg, i + (v + 1))
                        act.activation(xT[v], pT[u][:, 0:D].rearrange("p (k t) -> p k t", k=KD),
                                       ACT.Copy).then_inc(s_xt, 1)
                        if shared:
                            act.activation(xT_all[:, :, ds(i * P + v * P, P)],
                                           pT[u][:, 0:D].rearrange("p (k t) -> p k t", k=KD),
                                           ACT.Copy).then_inc(s_xta, 1)
            act.wait_ge(s_d, 1)
            act.activation(wexp[:], wexp[:], ACT.Exp).then_inc(s_we, 1)
            if shared:
                with act.Fori(0, NB * 2 - 1, 2) as q:
                    for f in range(2):
                        act.wait_ge(s_sgu, q + (f + 1))
                        act.wait_ge(s_sh, q + (f + 1))
                        act.activation(ssil[:, f, :], bank[4 + f][:], ACT.Silu).then_inc(s_ssil, 1)

        @blk.tensor
        def _(pe):
            pe.wait_ge(s_wr, 16 * (3 if shared else 2))
            pe.sem_inc(s_tr, UNROLL)
            pe.sem_inc(s_lg, 2 * UNROLL)

            def to_columns(i):
                for u in range(UNROLL):
                    pe.wait_ge(s_xn, i + (u + 1))
                    pe.wait_ge(s_xt, i + (u + 1))
                    if shared:
                        pe.wait_ge(s_xta, i + (u + 1))
                    for k in range(KD):
                        mm = pe.transpose(pT[u][:, k * P:(k + 1) * P], xn_t[u][:, k * P:(k + 1) * P],
                                          K["ident"])
                    mm.then_inc(s_tr, 1)

            def logits(i, half):
                for u in range(UNROLL):
                    pe.wait_ge(s_xt, i + (u + 1 + UNROLL))
                    for k in range(KD):
                        mm = pe.matmul(bank[2][:, ds(i * E + u * E, E)], xT[half * UNROLL + u][:, k, :], wr[:, k, :],
                                       start=(k == 0), stop=(k == KD - 1))
                    mm.then_inc(s_lg, 1)

            to_columns(0)
            to_columns(UNROLL)
            logits(0, 0)
            with pe.Fori(2 * UNROLL, NT - 2 * UNROLL + 1, 2 * UNROLL) as i:
                for half in range(2):
                    to_columns(i + half * UNROLL)
                    logits(i + (half - 1) * UNROLL, 1 - half)
            logits(NT - UNROLL, 1)
            pe.wait_ge(s_both, 1)
            if shared:
                pe.wait_ge(s_xta, NT + UNROLL)
            pe.matmul(bank[0][:, 0:NT * E], R["before"], both[:].rearrange("p i e -> p (i e)"),
                      start=True, stop=True)
            pe.matmul(bank[1][:, 0:NT * E], R["ones"], both[:].rearrange("p i e -> p (i e)"),
                      start=True, stop=True).then_inc(s_cnt, 1)
            if shared:
                pe.wait_ge(s_w, 64)

                def gate_up(blk_i, f):
                    for half in range(2):
                        for k in range(KD):
                            mm = pe.matmul(bank[4 + 2 * half + f][:],
                                           wsgu[:, k, half * SHARED + f * P:half * SHARED + (f + 1) * P],
                                           xT_all[:, k, ds(blk_i * SEQ, SEQ)],
                                           start=(k == 0), stop=(k == KD - 1))
                    mm.then_inc(s_sgu, 1)

                pe.sem_inc(s_sdn, 1)
                with pe.Fori(0, NB, 1) as n:
                    for f in range(2):
                        pe.wait_ge(s_sh, n * 2 + (f + 1))
                        gate_up(n, f)
                    pe.wait_ge(s_sh, n * 2 + 4)
                    for m in range(TB):
                        pe.wait_ge(s_sacc, n * TB + (m + 1))
                        for f in range(2):
                            mm = pe.matmul(bank[2 + m % 2][:, 0:D],
                                           hs[:, f, m * P:(m + 1) * P], wsdn[:, f, :],
                                           start=(f == 0), stop=(f == 1))
                        mm.then_inc(s_sdn, 1)

        @blk.vector
        def _(dve):
            c = Chain(dve, s_ch)

            def stats_of(k):
                layer_norm_stats(dve, c, x_sb, stats, mean, var, (k * CHUNK, (k + 1) * CHUNK))
                dve.sem_inc(s_var, 1)

            stats_of(0)
            dve.sem_inc(s_cp, UNROLL)
            for k in range(NT // CHUNK):
                if k < NT // CHUNK - 1:
                    stats_of(k + 1)
                dve.wait_ge(s_root, k + 1)
                layer_norm_rstd(dve, c, var, root, rstd, stats[:, :, 0], (k * CHUNK, (k + 1) * CHUNK))
                with dve.Fori(k * CHUNK, (k + 1) * CHUNK - UNROLL + 1, UNROLL) as i:
                    for u in range(UNROLL):
                        dve.wait_ge(s_tr, i + (u + 1))
                        dve.wait_ge(s_cp, i + (u + 1))
                        dve.tensor_scalar(xn_t[u][:], x_sb[:, ds(i + u, 1), :].rearrange("p a d -> p (a d)"),
                                          mean[:, ds(i + u, 1)], rstd[:, ds(i + u, 1)],
                                          ALU.subtract, ALU.mult).then_inc(s_xn, 1)
                    for u in range(UNROLL):
                        dve.wait_ge(s_xn, i + (u + 1))
                        dve.tensor_copy(xn[:, ds(i + u, 1), :].rearrange("p a d -> p (a d)"),
                                        xn_t[u][:]).then_inc(s_cp, 1)
            dve.wait_ge(s_cp, NT + UNROLL)
            dve.wait_ge(s_lg, NT + 2 * UNROLL)
            lg = bank[2][:, 0:NT * E].rearrange("p (i e) -> p i e", e=E)
            full = [P, NT, E]
            dve.wait_ge(s_wr, 16 * (3 if shared else 2))
            if shared:
                c.link(dve.tensor_tensor(logit[:], lg, bcast(ebias[:].unsqueeze(1), full), ALU.add))
            else:
                c.link(dve.tensor_copy(logit[:], lg))
            number = bcast(R["e_less"][:, 0:E].unsqueeze(1), full)
            for k in range(2):
                c.link(dve.tensor_reduce(best[k][:], logit[:], AX.X, ALU.max))
                c.link(dve.tensor_tensor(work[:], logit[:], bcast(best[k][:].unsqueeze(2), full), ALU.is_equal))
                c.link(dve.tensor_tensor(work[:], work[:], number, ALU.mult))
                c.link(dve.tensor_reduce(first[:], work[:], AX.X, ALU.min))
                c.link(dve.tensor_tensor(hot[k][:], number, bcast(first[:].unsqueeze(2), full), ALU.is_equal))
                if k == 0:
                    c.link(dve.scalar_tensor_tensor(out=logit[:], in0=hot[0][:], scalar=MASKED, in1=logit[:],
                                                    op0=ALU.mult, op1=ALU.add))
            dve.tensor_tensor(both[:], hot[0][:], hot[1][:], ALU.add).then_inc(s_both, 1)
            dve.tensor_tensor(wexp[:], best[1][:], best[0][:], ALU.subtract).then_inc(s_d, 1)
            dve.wait_ge(s_cnt, 1)
            c.link(dve.tensor_copy(count[:], bank[1][:, 0:NT * E].rearrange("p (i e) -> p e i", e=E)))
            c.link(dve.tensor_tensor_scan(upto[:].rearrange("p e i -> p (e i)"), R["restart"][:, 0:E * NT],
                                          count[:].rearrange("p e i -> p (e i)"), 0.0, ALU.mult, ALU.add))
            c.link(dve.tensor_tensor(work[:].rearrange("p i e -> p (i e)").rearrange("p (e i) -> p e i", e=E),
                                     bcast(upto[:, :, NT - 1:NT], [P, E, NT]),
                                     bcast(R["tile_start"].unsqueeze(1), [P, E, NT]), ALU.is_gt))
            c.link(dve.tensor_reduce(tiles[:], work[:].rearrange("p i e -> p (i e)").rearrange("p (e i) -> p e i", e=E),
                                     AX.X, ALU.add))
            c.link(dve.tensor_tensor_scan(tiles_upto[:], R["ones"][:, 0:E], tiles[:], 0.0, ALU.mult, ALU.add))
            c.link(dve.tensor_tensor(base[:], tiles_upto[:], tiles[:], ALU.subtract))
            c.link(dve.tensor_scalar(base[:], base[:], float(P), None, ALU.mult))
            c.link(dve.tensor_tensor(upto[:], upto[:], count[:], ALU.subtract))
            c.link(dve.tensor_tensor(upto[:], upto[:], bcast(base[:].unsqueeze(2), [P, E, NT]), ALU.add))
            c.link(dve.tensor_tensor(logit[:], bank[0][:, 0:NT * E].rearrange("p (i e) -> p i e", e=E),
                                     upto[:].rearrange("p e i -> p i e"), ALU.add))
            for k in range(2):
                c.link(dve.tensor_tensor(work[:], hot[k][:], logit[:], ALU.mult))
                c.link(dve.tensor_reduce(placef[:], work[:], AX.X, ALU.add))
                c.link(dve.tensor_copy(place[k][:], placef[:]))
            dve.sem_inc(s_place, 1)
            c.link(dve.tensor_tensor(owner_cmp[:], bcast(tiles_upto[:].unsqueeze(1), [P, NJ, E]),
                                     bcast(R["j"][:, 0:NJ].unsqueeze(2), [P, NJ, E]), ALU.is_le))
            c.link(dve.tensor_reduce(ownerf[:], owner_cmp[:], AX.X, ALU.add))
            c.link(dve.tensor_scalar(owner[:], ownerf[:], float(E - 1), None, ALU.min))
            dve.wait_ge(s_we, 1)
            c.link(dve.tensor_scalar(wsum[:], wexp[:], 1.0, None, ALU.add))
            c.link(dve.reciprocal(wsum[:], wsum[:]))
            c.link(dve.tensor_scalar(share[0][:], wsum[:], 0.5, None, ALU.mult))
            c.link(dve.tensor_tensor(share[1][:], share[0][:], wexp[:], ALU.mult))
            if shared:
                dve.sem_inc(s_sh, 2)
                dve.sem_inc(s_sacc, 2)
                with dve.Fori(0, NB, 1) as n:
                    for f in range(2):
                        dve.wait_ge(s_ssil, n * 2 + (f + 1))
                        dve.wait_ge(s_sdn, n * TB + 1)
                        dve.tensor_tensor(hs[:, f, :], ssil[:, f, :], bank[6 + f][:],
                                          ALU.mult).then_inc(s_sh, 1)
                    for m in range(TB):
                        dve.wait_ge(s_sdn, n * TB + (m + 2))
                        row = x_sb[:, ds(n * TB + m, 1), :].rearrange("p a d -> p (a d)")
                        dve.scalar_tensor_tensor(out=row, in0=bank[2 + m % 2][:, 0:D],
                                                 scalar=0.5, in1=row, op0=ALU.mult,
                                                 op1=ALU.add).then_inc(s_sacc, 1)

        routing.__exit__(None, None, None)

        s_in = [sem(f"x_in{b}") for b in range(UNROLL)]
        s_str = sem("xs_transposed")
        s_sxt = sem("xsT_ready")
        s_gu = sem("gate_up_done")
        s_pre = sem("pre_read")
        s_gate = sem("gate_ready")
        s_sig = sem("sigmoid_done")
        s_hid = sem("hidden_ready")
        s_glu = sem("glu_ready")
        s_upr = sem("up_ready")
        s_htr = sem("hidden_transposed")
        s_hT = sem("hidT_ready")
        s_dn = sem("down_done")
        s_y = sem("y_ready")
        s_st = [sem(f"y_stored{q}") for q in range(2)]
        NH = NJ // UNROLL
        LEAD = 1
        TR, GU, HID, HT, DN = -LEAD, 0, 1, 2, UNROLL

        pX, pG, pH, pY = bank[0:2], bank[2:4], bank[4:6], bank[6:8]
        with nc.Block() as blk:
            @blk.sync
            def _(sp):
                def load(tile, b):
                    sp.dma_start(x_in[b][:], xs[ds(tile * P, P), :]).then_inc(s_in[b], 16)

                for b in range(UNROLL):
                    load(b, b)
                with sp.Fori(1, NH, 1) as h:
                    for b in range(UNROLL):
                        sp.wait_ge(s_str, h * UNROLL + (b + 1 - UNROLL))
                        load(h * UNROLL + b, b)

            @blk.gpsimd
            def _(pool):
                with pool.Fori(0, NH, 1) as h:
                    for q in range(2):
                        pool.wait_ge(s_y, h * UNROLL + (2 * q + 2))
                        pool.dma_start(ys[ds(h * (UNROLL * P) + q * (2 * P), 2 * P), :]
                                       .rearrange("(r p) d -> p r d", p=P), y_out[q][:]).then_inc(s_st[q], 16)
                for q in range(2):
                    pool.wait_ge(s_st[q], 16 * NH)

            def owners(engine, s, lag):
                _, values = nc.values_load_multi_w_load_instructions(
                    owner[0:1, ds(s - lag, UNROLL)], engines=(engine,), min_val=0, max_val=E - 1,
                    skip_runtime_bounds_check_because="at most E - 1 by the routing")
                return values

            def of_expert(w, e):
                return w[:, ds(e, 1), :].rearrange("p a n -> p (a n)")

            @blk.tensor
            def _(pe):
                loaded = {}

                def body(s, b):
                    if b == 0:
                        for lag in (GU, DN):
                            if within(s, lag, NJ):
                                loaded[lag] = owners(mybir.EngineType.PE, s, lag)
                    if within(s, TR, NJ):
                        j, v = s - TR, (b - TR) % UNROLL
                        pe.wait_ge(s_in[v], (j - v) * (16 // UNROLL) + 16)
                        if after(j, 2):
                            pe.wait_ge(s_sxt, j - 1)
                        for k in range(KD):
                            mm = pe.transpose(pX[v % 2][:, k * P:(k + 1) * P], x_in[v][:, k * P:(k + 1) * P],
                                              K["ident"])
                        mm.then_inc(s_str, 1)
                    if within(s, GU, NJ):
                        j, c = s - GU, (b - GU) % 2
                        pe.wait_ge(s_sxt, j + 1)
                        if after(j, 2):
                            pe.wait_ge(s_hid if shared else s_pre, j - 1)
                        for k in range(KD):
                            mm = pe.matmul(pG[c][:, 0:2 * F], xsT[c][:, k, :],
                                           of_expert(wgu[:, k], loaded[GU][b]),
                                           start=(k == 0), stop=(k == KD - 1))
                        mm.then_inc(s_gu, 1)
                    if within(s, HT, NJ):
                        j, c = s - HT, (b - HT) % 2
                        pe.wait_ge(s_hid, j + 1)
                        if after(j, 2):
                            pe.wait_ge(s_hT, j - 1)
                        pe.transpose(pH[c][:, 0:P], hid[c][:], K["ident"]).then_inc(s_htr, 1)
                    if within(s, DN, NJ):
                        j, c = s - DN, (b - DN) % 2
                        pe.wait_ge(s_hT, j + 1)
                        if after(j, 2):
                            pe.wait_ge(s_y, j - 1)
                        pe.matmul(pY[c][:, 0:D], hidT[c][:], of_expert(wdn, loaded[DN][b]),
                                  start=True, stop=True).then_inc(s_dn, 1)

                steps(pe, NJ, LEAD, DN, body)

            @blk.scalar
            def _(act):
                def body(s, b):
                    if within(s, TR, NJ):
                        j, c = s - TR, (b - TR) % 2
                        act.wait_ge(s_str, j + 1)
                        if after(j, 2):
                            act.wait_ge(s_gu, j - 1)
                        act.activation(xsT[c][:], pX[c][:, 0:D].rearrange("p (k t) -> p k t", k=KD),
                                       ACT.Copy).then_inc(s_sxt, 1)
                    if within(s, HT, NJ):
                        j, c = s - HT, (b - HT) % 2
                        act.wait_ge(s_htr, j + 1)
                        if after(j, 2):
                            act.wait_ge(s_dn, j - 1)
                        act.activation(hidT[c][:], pH[c][:, 0:P], ACT.Copy).then_inc(s_hT, 1)
                    if within(s, GU, NJ):
                        j, c = s - GU, (b - GU) % 2
                        if shared:
                            act.wait_ge(s_gu, j + 1)
                            if after(j, 2):
                                act.wait_ge(s_hid, j - 1)
                            act.activation(sig[c][:], pG[c][:, 0:F], ACT.Silu).then_inc(s_sig, 1)
                        else:
                            act.wait_ge(s_gate, j + 1)
                            if after(j, 2):
                                act.wait_ge(s_glu, j - 1)
                            act.activation(sig[c][:], gate[c][:], ACT.Sigmoid, scale=ALPHA).then_inc(s_sig, 1)

                steps(act, NJ, LEAD, HT, body)

            @blk.vector
            def _(dve):
                loaded = {}

                def result(s, b):
                    if within(s, DN, NJ):
                        j, v = s - DN, (b - DN) % UNROLL
                        dve.wait_ge(s_dn, j + 1)
                        if v % 2 == 0 and after(j, UNROLL):
                            dve.wait_ge(s_st[v // 2], (j - v) * (16 // UNROLL))
                        out = y_out[v // 2][:, v % 2, :]
                        if shared:
                            dve.tensor_copy(out, pY[v % 2][:, 0:D]).then_inc(s_y, 1)
                        else:
                            dve.tensor_tensor(out, pY[v % 2][:, 0:D], of_expert(bdn, loaded[DN][b]),
                                              ALU.add).then_inc(s_y, 1)

                def hidden(s, b):
                    if within(s, HID, NJ):
                        j, c = s - HID, (b - HID) % 2
                        dve.wait_ge(s_sig, j + 1)
                        dve.wait_ge(s_gate, j + 1)
                        dve.tensor_tensor(glu[c][:], gate[c][:], sig[c][:], ALU.mult).then_inc(s_glu, 1)
                        dve.wait_ge(s_glu, j + 1)
                        dve.wait_ge(s_upr, j + 1)
                        if after(j, 2):
                            dve.wait_ge(s_htr, j - 1)
                        dve.scalar_tensor_tensor(out=hid[c][:], in0=up[c][:], scalar=1.0, in1=glu[c][:],
                                                 op0=ALU.add, op1=ALU.mult).then_inc(s_hid, 1)
                    if within(s, GU, NJ):
                        j, c = s - GU, (b - GU) % 2
                        dve.wait_ge(s_gu, j + 1)
                        dve.tensor_tensor(pre[c][:], pG[c][:, 0:2 * F], of_expert(bgu, loaded[GU][b]),
                                          ALU.add).then_inc(s_pre, 1)
                        dve.wait_ge(s_pre, j + 1)
                        if after(j, 2):
                            dve.wait_ge(s_glu, j - 1)
                            dve.wait_ge(s_hid, j - 1)
                        dve.tensor_scalar(gate[c][:], pre[c][:, 0:F], LIMIT, None, ALU.min).then_inc(s_gate, 1)
                        dve.tensor_scalar(up[c][:], pre[c][:, F:2 * F], LIMIT, -LIMIT, ALU.min,
                                          ALU.max).then_inc(s_upr, 1)

                def hidden_shared(s, b):
                    if within(s, HID, NJ):
                        j, c = s - HID, (b - HID) % 2
                        dve.wait_ge(s_sig, j + 1)
                        if after(j, 2):
                            dve.wait_ge(s_htr, j - 1)
                        dve.tensor_tensor(hid[c][:], sig[c][:], pG[c][:, F:2 * F],
                                          ALU.mult).then_inc(s_hid, 1)

                def body(s, b):
                    if b == 0 and not shared:
                        for lag in (GU, DN):
                            if within(s, lag, NJ):
                                loaded[lag] = owners(mybir.EngineType.DVE, s, lag)
                    (hidden_shared if shared else hidden)(s, b)
                    result(s, b)

                steps(dve, NJ, LEAD, DN, body)

        s_got = [sem(f"y_got{r}") for r in range(RING)]
        s_half = sem("first_added")
        s_used = sem("second_added")
        s_out = sem("x_stored")
        with nc.Block() as blk:
            if out is not None:
                @blk.sync
                def _(sp):
                    tiles = out.rearrange("(i p) d -> p i d", p=P)
                    for q in range(NT // RING):
                        sp.wait_ge(s_used, (q + 1) * RING)
                        sp.dma_start(tiles[:, q * RING:(q + 1) * RING, :],
                                     x_sb[:, q * RING:(q + 1) * RING, :]).then_inc(s_out, 16)
                    sp.wait_ge(s_out, 16 * (NT // RING))

            @blk.gpsimd
            def _(pool):
                for i in range(NT):
                    if i >= RING:
                        pool.wait_ge(s_used, i - RING + 1)
                    for k in range(2):
                        pool.indirect_dma_start(
                            y_got[i % RING][:, k, :], None, ys[0:NJ * P, :],
                            bass.IndirectOffsetOnAxis(ap=place[k][:, i:i + 1], axis=0)
                        ).then_inc(s_got[i % RING], 16)

            @blk.vector
            def _(dve):
                with dve.Fori(0, NT // RING, 1) as q:
                    for r in range(RING):
                        row = x_sb[:, ds(q * RING + r, 1), :].rearrange("p a d -> p (a d)")
                        dve.wait_ge(s_got[r], q * 32 + 32)
                        for k in range(2):
                            if k == 1:
                                dve.wait_ge(s_half, q * RING + (r + 1))
                            dve.scalar_tensor_tensor(
                                out=row, in0=y_got[r][:, k, :], scalar=share[k][:, ds(q * RING + r, 1)],
                                in1=row, op0=ALU.mult, op1=ALU.add).then_inc(s_used if k else s_half, 1)


CH = 512
CB = CH // P
NS = 16
RANK = 64
TAPS = 4
LOG1P = (0.999999806, -0.499974054, 0.3327548, -0.24495463, 0.177452402, -0.107681677, 0.0440895953,
         -0.00853919577)


def batch_row_loop(eng, step):
    HEAD = 3
    for n in range(HEAD):
        step(0, 0, n, False, True, True)
    with eng.Fori(0, BATCH // 2 - 1, 1) as q:
        for par in range(2):
            for n in range(HEAD, NS):
                step(2 * q + par, par, n, True, True, True)
            for n in range(HEAD):
                step(2 * q + (par + 1), 1 - par, n, True, True, True)
    for b in (BATCH - 2, BATCH - 1):
        for n in range(HEAD, NS):
            step(b, b % 2, n, True, True, b < BATCH - 1)
        for n in range(HEAD):
            step(b + 1, 1 - b % 2, n, True, b < BATCH - 1, False)


def mamba_phase(nc, x_sb, K, A):
    with ExitStack() as ctx:
        def sb(name, shape, dt=F32):
            return ctx.enter_context(nc.sbuf_tensor(f"ssm_{name}", shape, dt))

        def sem(name):
            return nc.alloc_semaphore(f"ssm_{name}")

        win = sb("win", [P, KD, 2 * CH])
        wbd = sb("wbd", [P, KD, P])
        wdt = sb("wdt", [P, CH])
        wout = sb("wout", [P, CB, D])
        col = sb("col", [P, 3 * CB + 2 + CB * TAPS])
        bias_v, bias_x, bias_dt = (col[:, k * CB:(k + 1) * CB] for k in range(3))
        bias_bd = sb("bias_bd", [P, 1])
        tap = col[:, 3 * CB + 2:]
        decay = sb("decay", [P, CB, NS])
        cmat = sb("cmat", [P, CB, NS])
        cdiag = sb("cdiag", [P, NS, CB, P])
        bout = sb("bout", [P, D])
        mean, var, root, rstd = (sb(k, [P, NT]) for k in ("mean", "var", "root", "rstd"))
        xn_t = [sb(f"xn_t{k}", [P, D]) for k in range(2)]
        xnT = sb("xnT", [P, KD, SEQ])
        xpad = sb("xpad", [P, CB, TAPS - 1 + SEQ])
        sv = [sb(f"sv{k}", [P, CB, SEQ]) for k in range(2)]
        delta = [sb(f"delta{k}", [P, CB, SEQ]) for k in range(2)]
        dx = [sb(f"dx{k}", [P, CB, SEQ]) for k in range(2)]
        bd = [sb(f"bd{k}", [P, SEQ]) for k in range(2)]
        ex = sb("ex", [P, 2, SEQ])
        stats = ex[:, 0, 0:NT * 6].rearrange("p (i s) -> p i s", s=6)
        log = sb("log", [P, 2, SEQ])
        tmp = sb("tmp", [P, SEQ])
        dA = [sb(f"dA{k}", [P, CB, SEQ]) for k in range(2)]
        RH = 4
        hs = [sb(f"h{k}", [P, CB, SEQ]) for k in range(RH)]

        y_ps = ctx.enter_context(nc.psum_tensor("ssm_y_ps", [P, CB, SEQ], F32))
        b_ps = [ctx.enter_context(nc.psum_tensor(f"ssm_b_ps{k}", [P, SEQ], F32)) for k in range(2)]
        pj = [ctx.enter_context(nc.psum_tensor(f"ssm_pj{k}", [P, SEQ], F32)) for k in range(2)]

        s_w = sem("weights_in")
        s_col = sem("columns_in")
        s_late = sem("late_weights_in")
        s_chain = sem("dve_chain")
        s_var = sem("var_ready")
        s_root = sem("root_ready")
        s_dec = sem("decay_exp")
        s_neg = sem("decay_ready")
        s_set = sem("pads_ready")
        s_cd = sem("cdiag_ready")
        s_bias = sem("bias_ready")
        s_xn = sem("xn_ready")
        s_pj = sem("projected")
        s_ev = sem("evacuated_plus_1")
        s_conv = sem("convolved")
        s_silu = sem("silus_done")
        s_abs = sem("abs_done")
        s_ex = sem("ex_ready")
        s_poly = sem("log_steps")
        s_log = sem("log_ready")
        s_pool = sem("pool_chain")
        s_held = sem("held")
        s_delta = sem("delta_ready")
        s_dx = sem("dx_ready")
        s_xb = sem("bias_added")
        s_bb = sem("b_spread")
        s_da = sem("dA_ready")
        s_dbx = sem("dbx_ready_plus_17")
        s_scan = sem("scans_plus_1")
        s_diag = sem("summed_plus_3")
        s_g = sem("gated")
        s_op = sem("out_projected")
        s_xadd = sem("x_added")


        PIECES = [("T", 0, 0), ("T", 1, 0), ("T", 2, 1), ("T", 3, 1), ("X", 0, 2), ("BD", 0, 2), ("X", 1, 3),
                  ("DT", 0, 3), ("X", 2, 4), ("DT", 1, 4), ("X", 3, 5), ("V", 0, 6), ("V", 1, 7),
                  ("DT", 2, 8), ("DT", 3, 8), ("V", 2, 9), ("V", 3, 10)]
        USES = len(PIECES)
        USE = {(kind, k): u for u, (kind, k, _) in enumerate(PIECES)}
        POOL = ([("conv", c) for c in range(CB)] + [("delta", c) for c in range(CB)]
                + [("dx", c) for c in range(CB)] + [("xb", m) for m in range(TB)])
        CHAIN = CB * (2 * TAPS - 2)
        LOG_STEPS = len(LOG1P)
        LOG_PER, LOG_AT = 3, (6, 10)
        SILU = 12

        def bank_of(f, fpar, u):
            return pj[(fpar * USES + u) % 2]

        with nc.Block() as blk:
            @blk.sync
            def _(sp):
                for group, loads in ((s_col, ((col, "col"), (decay, "alog"), (cmat, "cmat"))),
                                     (s_w, ((win, "win"), (wbd, "wbd"), (wdt, "wdt"))), (s_late, ((wout, "wout"),))):
                    for dst, name in loads:
                        sp.dma_start(dst[:], A["ssm_" + name]).then_inc(group, 16)
                sp.dma_start(bout[:], A["ssm_bout"].partition_broadcast(P)).then_inc(s_late, 16)
                sp.wait_ge(s_w, 48)
                sp.wait_ge(s_late, 32)

            @blk.gpsimd
            def _(pool):
                pool.wait_ge(s_col, 48)

                def conv(f, fpar, c, k0):
                    pool.wait_ge(s_ev, f * USES + USE["X", c] + 2)
                    if c == 0:
                        pool.wait_ge(s_dbx, f * NS + 1)
                    acc = dx[fpar][:, c, :]
                    for k in range(TAPS):
                        src = xpad[:, c, k:k + SEQ]
                        n = k0 + 2 * k
                        if k == 0:
                            pool.sem_inc(s_held, 1)
                        if k == 0:
                            pool.tensor_scalar(acc, src, tap[:, c * TAPS:c * TAPS + 1], 0.0,
                                               ALU.mult, ALU.add).then_inc(s_pool, 1)
                            continue
                        pool.sem_inc(s_held, 1)
                        pool.tensor_scalar(tmp[:], src, tap[:, c * TAPS + k:c * TAPS + k + 1], 0.0,
                                           ALU.mult, ALU.add).then_inc(s_pool, 1)
                        pool.wait_ge(s_pool, f * CHAIN + n)
                        ins = pool.tensor_tensor(acc, acc, tmp[:], ALU.add)
                        ins.then_inc(s_conv if k == TAPS - 1 else s_pool, 1)
                        if k < TAPS - 1:
                            pool.wait_ge(s_pool, f * CHAIN + n + 1)
                        else:
                            pool.wait_ge(s_conv, f * CB + c + 1)

                def soft(f, fpar, c):
                    pool.wait_ge(s_log, f * 2 + c // 2 + 1)
                    pool.tensor_tensor(delta[fpar][:, c, :], delta[fpar][:, c, :], log[:, c % 2, :],
                                       ALU.add).then_inc(s_delta, 1)
                    pool.wait_ge(s_delta, f * CB + c + 1)

                def row(f, fpar):
                    k0 = 0
                    for kind, k in POOL:
                        if kind == "conv":
                            conv(f, fpar, k, k0)
                            k0 += 2 * TAPS - 2
                        elif kind == "delta":
                            soft(f, fpar, k)
                        elif kind == "dx":
                            pool.wait_ge(s_silu, f * 2 + 2)
                            pool.tensor_tensor(dx[fpar][:, k, :], dx[fpar][:, k, :], delta[fpar][:, k, :],
                                               ALU.mult).then_inc(s_dx, 1)
                        else:
                            pool.wait_ge(s_xn, f * TB + k + 1)
                            x_row = x_sb[:, ds(f * TB + k, 1), :].rearrange("p a d -> p (a d)")
                            pool.tensor_tensor(x_row, x_row, bout[:], ALU.add).then_inc(s_xb, 1)
                    assert k0 == CHAIN

                pool.wait_ge(s_set, 1)
                pool.wait_ge(s_late, 32)
                with pool.Fori(0, BATCH // 2, 1) as q:
                    for fpar in range(2):
                        row(2 * q + fpar, fpar)

            @blk.scalar
            def _(act):
                act.wait_ge(s_col, 48)
                for n in range(NS):
                    for c in range(CB):
                        ins = act.activation(cdiag[:, n, c, :], K["ident"], ACT.Identity,
                                             scale=cmat[:, c, n:n + 1])
                ins.then_inc(s_cd, 1)
                act.wait_ge(s_var, 1)
                act.activation(root[:], var[:], ACT.Sqrt).then_inc(s_root, 1)
                act.activation(decay[:], decay[:], ACT.Exp).then_inc(s_dec, 1)
                act.activation(bias_bd[:], col[:, 3 * CB:3 * CB + 1], ACT.Identity,
                               bias=col[:, 3 * CB + 1:3 * CB + 2]).then_inc(s_bias, 1)
                act.wait_ge(s_neg, 1)
                act.wait_ge(s_set, 1)
                act.wait_ge(s_bias, 1)
                act.sem_inc(s_ev, 1)
                act.preload_act_table_set("natural_log_exp_and_others")

                def piece(f, fpar, u):
                    kind, k, _ = PIECES[u]
                    src = bank_of(f, fpar, u)
                    old = not (isinstance(f, int) and f < 2)
                    act.wait_ge(s_pj, f * USES + u + 1)
                    if kind == "T":
                        act.activation(xnT[:, :, k * P:(k + 1) * P],
                                       src[:, 0:D].rearrange("p (k t) -> p k t", k=KD),
                                       ACT.Copy).then_inc(s_ev, 1)
                    elif kind == "X":
                        act.wait_ge(s_conv, f * CB)
                        act.activation(xpad[:, k, TAPS - 1:], src[:], ACT.Identity,
                                       bias=bias_x[:, k:k + 1]).then_inc(s_ev, 1)
                    elif kind == "V":
                        if old and k == 0:
                            act.wait_ge(s_op, (f - 1) * TB)
                        act.activation(sv[fpar][:, k, :], src[:], ACT.Identity,
                                       bias=bias_v[:, k:k + 1]).then_inc(s_ev, 1)
                    elif kind == "BD":
                        if old:
                            act.wait_ge(s_bb, (f - 1) * NS)
                        act.activation(bd[fpar][:], src[:], ACT.Identity,
                                       bias=bias_bd[:]).then_inc(s_ev, 1)
                    else:
                        act.wait_ge(s_delta, f * CB + k - k % 2)
                        if old and k == 0:
                            act.wait_ge(s_da, (f - 1) * NS)
                            act.wait_ge(s_dx, (f - 1) * CB)
                        act.activation(ex[:, k % 2, :], src[:], ACT.Abs,
                                       bias=bias_dt[:, k:k + 1]).then_inc(s_abs, 1)
                        act.activation(delta[fpar][:, k, :], src[:], ACT.Relu,
                                       bias=bias_dt[:, k:k + 1]).then_inc(s_ev, 1)
                        act.wait_ge(s_abs, f * CB + k + 1)
                        act.activation(ex[:, k % 2, :], ex[:, k % 2, :], ACT.Exp,
                                       scale=-1.0).then_inc(s_ex, 1)

                def silus(f, fpar):
                    act.wait_ge(s_ev, f * USES + USE["V", CB - 1] + 2)
                    act.activation(sv[fpar][:], sv[fpar][:], ACT.Silu).then_inc(s_silu, 1)
                    act.wait_ge(s_conv, (f + 1) * CB)
                    act.activation(dx[fpar][:], dx[fpar][:], ACT.Silu).then_inc(s_silu, 1)
                    act.preload_act_table_set("natural_log_exp_and_others")

                for u in range(USES):
                    piece(0, 0, u)
                silus(0, 0)

                def step(b, par, n, prev, main, front):
                    if main:
                        if n == 0:
                            act.wait_ge(s_delta, (b + 1) * CB)
                        act.wait_ge(s_scan, b * NS + n)
                        for c in range(CB):
                            ins = act.activation(dA[n % 2][:, c, 1:], delta[par][:, c, 1:], ACT.Exp,
                                                 scale=decay[:, c, n:n + 1])
                        ins.then_inc(s_da, 1)
                    if front:
                        for u, (_, _, at) in enumerate(PIECES):
                            if at == n - 1 or (at == NS - 1 and n == NS - 1):
                                piece(b + 1, 1 - par, u)
                        if n == SILU:
                            silus(b + 1, 1 - par)

                batch_row_loop(act, step)

            @blk.tensor
            def _(pe):
                def piece(f, fpar, u):
                    kind, k, _ = PIECES[u]
                    dst = bank_of(f, fpar, u)
                    pe.wait_ge(s_ev, f * USES + u)
                    if kind == "T":
                        pe.wait_ge(s_xn, f * TB + k + 1)
                        for kd in range(KD):
                            mm = pe.transpose(dst[:, kd * P:(kd + 1) * P], xn_t[k % 2][:, kd * P:(kd + 1) * P],
                                              K["ident"])
                    elif kind == "DT":
                        pe.wait_ge(s_ev, f * USES + USE["BD", 0] + 2)
                        mm = pe.matmul(dst[:], wdt[RANK:P, k * P:(k + 1) * P], bd[fpar][RANK:P, :],
                                       start=True, stop=True)
                    else:
                        if u == TB:
                            pe.wait_ge(s_ev, f * USES + TB + 1)
                        w = wbd if kind == "BD" else win
                        at = {"V": k * P, "X": CH + k * P, "BD": 0}[kind]
                        for kd in range(KD):
                            mm = pe.matmul(dst[:], w[:, kd, at:at + P], xnT[:, kd, :],
                                           start=(kd == 0), stop=(kd == KD - 1))
                    mm.then_inc(s_pj, 1)

                def spread(b, par, n):
                    if n == 0:
                        pe.wait_ge(s_ev, b * USES + USE["BD", 0] + 2)
                    pe.wait_ge(s_dbx, b * NS + NS + n)
                    pe.matmul(b_ps[n % 2][:], K["ident"][0:NS, n:n + 1].broadcast_to([NS, P]),
                              bd[par][0:NS, :], start=True, stop=True).then_inc(s_bb, 1)

                def sums(b, par, n):
                    pe.wait_ge(s_scan, b * NS + n + 2)
                    for c in range(CB):
                        if n == 0 and not (isinstance(b, int) and b == 0):
                            pe.wait_ge(s_xadd, b * TB - TB + c + 1)
                        mm = pe.matmul(y_ps[:, c, :], cdiag[:, n, c, :], hs[n % RH][:, c, :],
                                       start=(n == 0), stop=(n == NS - 1))
                    mm.then_inc(s_diag, 1)

                def project(b, par):
                    pe.wait_ge(s_g, b + 1)
                    for m in range(TB):
                        for c in range(CB):
                            mm = pe.matmul(y_ps[:, m, 0:D], sv[par][:, c, m * P:(m + 1) * P], wout[:, c, :],
                                           start=(c == 0), stop=(c == CB - 1))
                        mm.then_inc(s_op, 1)

                pe.wait_ge(s_w, 48)
                for u in range(USES):
                    piece(0, 0, u)
                spread(0, 0, 0)
                spread(0, 0, 1)
                pe.wait_ge(s_cd, 1)
                pe.wait_ge(s_late, 32)

                def step(b, par, n, prev, main, front):
                    if n == 0:
                        if prev:
                            sums(b - 1, 1 - par, NS - 1)
                    else:
                        if n == 1 and prev:
                            project(b - 1, 1 - par)
                        if main:
                            sums(b, par, n - 1)
                    if main and n < NS - 2:
                        spread(b, par, n + 2)
                    if front:
                        for u, (_, _, at) in enumerate(PIECES):
                            if at == n:
                                piece(b + 1, 1 - par, u)
                        if n >= NS - 2:
                            spread(b + 1, 1 - par, n + 2 - NS)

                batch_row_loop(pe, step)

            @blk.vector
            def _(dve):
                c = Chain(dve, s_chain)
                for k in range(2):
                    dve.memset(dA[k][:, :, 0:1], 0.0).then_inc(c.sem, 1)
                dve.memset(xpad[:, :, 0:TAPS - 1], 0.0).then_inc(c.sem, 1)
                c.n = 3
                layer_norm_stats(dve, c, x_sb, stats, mean, var)
                dve.sem_inc(s_set, 1)
                dve.sem_inc(s_var, 1)
                dve.sem_inc(s_scan, 1)
                dve.sem_inc(s_dbx, NS + 1)
                dve.sem_inc(s_diag, 3)
                dve.wait_ge(s_dec, 1)
                dve.tensor_scalar(decay[:], decay[:], -1.0, None, ALU.mult).then_inc(s_neg, 1)
                dve.wait_ge(s_root, 1)
                layer_norm_rstd(dve, c, var, root, rstd, stats[:, :, 0])

                def norm(f, m):
                    dve.wait_ge(s_pj, f * USES + max(m - 1, 0))
                    dve.tensor_scalar(xn_t[m % 2][:],
                                      x_sb[:, ds(f * TB + m, 1), :].rearrange("p a d -> p (a d)"),
                                      mean[:, ds(f * TB + m, 1)], rstd[:, ds(f * TB + m, 1)],
                                      ALU.subtract, ALU.mult).then_inc(s_xn, 1)

                def dbx(b, par, n):
                    if n == 0:
                        dve.wait_ge(s_dx, (b + 1) * CB)
                    dve.wait_ge(s_bb, b * NS + n + 1)
                    dve.wait_ge(s_diag, b * NS + n)
                    dve.tensor_tensor(hs[n % RH][:], dx[par][:],
                                      b_ps[n % 2][:].unsqueeze(1).broadcast_to([P, CB, SEQ]),
                                      ALU.mult).then_inc(s_dbx, 1)

                def scan(b, n):
                    dve.wait_ge(s_da, b * NS + n + 1)
                    dve.wait_ge(s_dbx, b * NS + NS + n + 2)
                    h = hs[n % RH][:].rearrange("p c t -> p (c t)")
                    dve.tensor_tensor_scan(h, dA[n % 2][:].rearrange("p c t -> p (c t)"), h, 0.0,
                                           ALU.mult, ALU.add).then_inc(s_scan, 1)

                def log1p(f, g, k):
                    if k == 0:
                        dve.wait_ge(s_ex, f * CB + 2 * g + 2)
                        dve.wait_ge(s_delta, f * CB + 2 * g)
                        ins = dve.tensor_scalar(log[:], ex[:], LOG1P[-1], LOG1P[-2], ALU.mult, ALU.add)
                    else:
                        dve.wait_ge(s_poly, f * (2 * LOG_STEPS) + g * LOG_STEPS + k)
                        if k == 1:
                            ins = dve.tensor_tensor(log[:], log[:], ex[:], ALU.mult)
                        else:
                            ins = dve.scalar_tensor_tensor(out=log[:], in0=log[:], scalar=LOG1P[-1 - k], in1=ex[:],
                                                           op0=ALU.add, op1=ALU.mult)
                    ins.then_inc(s_poly, 1)
                    if k == LOG_STEPS - 1:
                        dve.wait_ge(s_poly, f * (2 * LOG_STEPS) + (g + 1) * LOG_STEPS)
                        dve.sem_inc(s_log, 1)

                def gated(b, par):
                    dve.wait_ge(s_diag, b * NS + NS + 3)
                    dve.wait_ge(s_silu, b * 2 + 1)
                    dve.tensor_tensor(sv[par][:], sv[par][:], y_ps[:], ALU.mult).then_inc(s_g, 1)

                def added(b, tiles):
                    for m in tiles:
                        dve.wait_ge(s_op, b * TB + m + 1)
                        dve.wait_ge(s_xb, b * TB + m + 1)
                        x_row = x_sb[:, ds(b * TB + m, 1), :].rearrange("p a d -> p (a d)")
                        dve.tensor_tensor(x_row, x_row, y_ps[:, m, 0:D], ALU.add).then_inc(s_xadd, 1)

                for m in range(TB):
                    norm(0, m)
                for g in range(2):
                    for k in range(LOG_STEPS):
                        log1p(0, g, k)

                def step(b, par, n, prev, main, front):
                    if main:
                        dbx(b, par, n)
                    if prev and n == 1:
                        gated(b - 1, 1 - par)
                    if prev and n == 2:
                        added(b - 1, range(TB // 2))
                    if n == 0:
                        if prev:
                            scan(b - 1, NS - 1)
                    elif main:
                        scan(b, n - 1)
                    if prev and n == 2:
                        added(b - 1, range(TB // 2, TB))
                    if front:
                        for kind, k, at in PIECES:
                            if kind == "T" and at == n:
                                norm(b + 1, k)
                        for g, start in enumerate(LOG_AT):
                            for k in range(LOG_STEPS):
                                if n == start + k // LOG_PER:
                                    log1p(b + 1, g, k)

                batch_row_loop(dve, step)


HEADS, HD = 16, 16
GROUP = 4
GROUPS = HEADS // GROUP
HP = P // GROUP


def attention_phase(nc, x_sb, K, A):
    with ExitStack() as ctx:
        def sb(name, shape, dt=F32):
            return ctx.enter_context(nc.sbuf_tensor(f"att_{name}", shape, dt))

        def ps(name, shape, dt=F32):
            return ctx.enter_context(nc.psum_tensor(f"att_{name}", shape, dt))

        def sem(name):
            return nc.alloc_semaphore(f"att_{name}")

        RT = 4
        wq, wk = (sb(k, [P, KD, GROUPS * P]) for k in ("wq", "wk"))
        wv = sb("wv", [P, KD, D])
        wo = sb("wo", [P, GROUPS, D])
        q_bias, k_bias = (sb(k, [P, GROUPS, SEQ]) for k in ("q_bias", "k_bias"))
        maskf = sb("maskf", [P, P])
        mask, identb = sb("mask", [P, P], BF16), sb("identb", [P, P], BF16)
        stats = sb("stats", [P, NT, 6])
        mean, var, root, rstd = (sb(k, [P, NT]) for k in ("mean", "var", "root", "rstd"))
        xn_t = [sb(f"xn_t{k}", [P, D]) for k in range(2)]
        xnT = sb("xnT", [P, KD, SEQ])
        qT = [sb(f"qT{k}", [P, SEQ]) for k in range(2)]
        kT = [sb(f"kT{k}", [P, SEQ]) for k in range(2)]
        v = [sb(f"v{k}", [P, TB, GROUP, HP]) for k in range(2)]
        prob = [sb(f"prob{k}", [P, GROUP, SEQ]) for k in range(2)]
        top = [sb(f"top{k}", [P, GROUP]) for k in range(2)]
        total = [sb(f"total{k}", [P, GROUP]) for k in range(2)]
        inv = sb("inv", [P, GROUP])
        inv_b = sb("inv_b", [P, GROUP, HP])
        inv_t = sb("inv_t", [P, P])
        probT = [sb(f"probT{k}", [P, GROUP, P]) for k in range(RT)]
        oT = sb("oT", [P, GROUPS, SEQ])

        sc = [ps(f"sc{j}", [P, SEQ]) for j in range(GROUP)]
        turn = [ps(f"turn{k}", [P, SEQ]) for k in range(2)]
        o_ps = ps("o_ps", [P, P])
        misc = ps("misc", [P, SEQ])

        s_w = sem("weights_in")
        s_chain = sem("dve_chain")
        s_var = sem("var_ready")
        s_root = sem("root_ready")
        s_c = sem("constants_ready")
        s_xn = sem("xn_ready")
        s_m = sem("misc_written")
        s_me = sem("misc_read")
        s_sc = sem("scores_ready")
        s_top = sem("top_ready")
        s_ex = sem("probs_ready")
        s_inv = sem("inv_ready")
        s_ib = sem("inv_b_ready")
        s_t = sem("turned")
        s_td = sem("turns_read_by_dve_plus_2")
        s_ta = sem("turns_read_by_act")
        s_pv = sem("pv_done_plus_4")
        s_at = sem("oT_ready_plus_1")


        UNITS = GROUPS * TB

        def uses(has_next):
            out = []
            for u in range(UNITS):
                g, i = divmod(u, TB)
                if i < 3 and (g < GROUPS - 1 or has_next):
                    out.append((u, "QKV"[i], (g + 1) % GROUPS))
                if g == GROUPS - 2 and i == 3 and has_next:
                    out += [(u, "T", m) for m in range(TB)]
                if u == UNITS - 1:
                    out += [(u, "out", m) for m in range(TB)]
            return out

        FIRST = [(None, "T", m) for m in range(TB)] + [(None, k, 0) for k in "QKV"]
        M0, MU = len(FIRST), len(uses(True))
        TURNS = [sum(k + 2 for k in range(u % TB)) + u // TB * 14 for u in range(UNITS)]
        PVS = [sum(k + 1 for k in range(u % TB)) + u // TB * 10 for u in range(UNITS)]
        NTURN, NPV = 14 * GROUPS, 10 * GROUPS
        ACT_TILES = (0,)
        BY_ACT = [kt in ACT_TILES and kt <= u % TB for u in range(UNITS) for kt in range(u % TB + 2)]

        def wait_read(eng, b, q):
            if q < 0:
                q, b = q + NTURN, b - 1
            if BY_ACT[q]:
                eng.wait_ge(s_ta, b * sum(BY_ACT) + (sum(BY_ACT[:q]) + 1))
            else:
                eng.wait_ge(s_td, b * (NTURN - sum(BY_ACT)) + (q - sum(BY_ACT[:q]) + 3))

        def rows_loop(eng, body):
            with eng.Fori(0, BATCH - 1, 1) as b:
                body(b, True)
            body(BATCH - 1, False)

        with nc.Block() as blk:
            @blk.sync
            def _(sp):
                for dst, name in ((wq, "wq"), (wk, "wk"), (wv, "wv"), (wo, "wo"), (q_bias, "q_bias"),
                                  (k_bias, "k_bias"), (maskf, "mask")):
                    sp.dma_start(dst[:], A["att_" + name]).then_inc(s_w, 16)
                sp.wait_ge(s_w, 112)

            @blk.scalar
            def _(act):
                act.wait_ge(s_var, 1)
                act.activation(root[:], var[:], ACT.Sqrt).then_inc(s_root, 1)
                act.wait_ge(s_w, 112)
                act.activation(mask[:], maskf[:], ACT.Copy).then_inc(s_c, 1)
                act.activation(identb[:], K["ident"], ACT.Copy).then_inc(s_c, 1)

                def tile_copy(at, m):
                    act.wait_ge(s_m, at + 1)
                    act.activation(xnT[:, :, m * P:(m + 1) * P],
                                   misc[:, 0:D].rearrange("p (k t) -> p k t", k=KD),
                                   ACT.Copy).then_inc(s_me, 1)

                ORDER = (("exp", 0), ("exp", 1), ("copy", 0), ("exp", 2), ("exp", 3))

                def exp(b, u, j):
                    i = u % TB
                    act.wait_ge(s_top, (b * UNITS + u) * GROUP + j + 1)
                    act.activation(prob[u % 2][:, j, 0:(i + 1) * P], sc[j][:, 0:(i + 1) * P], ACT.Exp,
                                   bias=top[u % 2][:, j:j + 1],
                                   accum_out=total[u % 2][:, j:j + 1]).then_inc(s_ex, 1)

                def turned(b, u, kt):
                    act.wait_ge(s_t, b * NTURN + TURNS[u] + kt + 1)
                    act.wait_ge(s_pv, b * NPV + PVS[u] + kt + 1)
                    act.activation(probT[(PVS[u] + kt) % RT][:].rearrange("p j t -> p (j t)"),
                                   turn[(TURNS[u] + kt) % 2][:], ACT.Copy).then_inc(s_ta, 1)

                for n, (_, kind, m) in enumerate(FIRST):
                    if kind == "T":
                        tile_copy(n, m)
                act.preload_act_table_set("exp_and_others")
                for j in range(GROUP):
                    exp(0, 0, j)

                def body(b, has_next):
                    for u in range(UNITS):
                        for kind, k in ORDER:
                            if kind == "copy":
                                if k <= u % TB:
                                    turned(b, u, k)
                            elif u < UNITS - 1:
                                exp(b, u + 1, k)
                            elif has_next:
                                exp(b + 1, 0, k)
                        for n, (at, kind, m) in enumerate(uses(has_next)):
                            if at == u and kind == "T":
                                tile_copy(b * MU + M0 + n, m)

                rows_loop(act, body)

            @blk.tensor
            def _(pe):
                def use(at, kind, k):
                    pe.wait_ge(s_me, at)
                    if kind == "T":
                        pe.wait_ge(s_xn, tiles_before(at) + k + 1)
                        for kd in range(KD):
                            mm = pe.transpose(misc[:, kd * P:(kd + 1) * P],
                                              xn_t[k % 2][:, kd * P:(kd + 1) * P], K["ident"])
                    elif kind in "QK":
                        w = wq if kind == "Q" else wk
                        for kd in range(KD):
                            mm = pe.matmul(misc[:], w[:, kd, k * P:(k + 1) * P], xnT[:, kd, :],
                                           start=(kd == 0), stop=(kd == KD - 1))
                    elif kind == "V":
                        for m in range(TB):
                            for kd in range(KD):
                                mm = pe.matmul(misc[:, m * GROUP * HD:(m + 1) * GROUP * HD],
                                               xnT[:, kd, m * P:(m + 1) * P],
                                               wv[:, kd, k * GROUP * HD:(k + 1) * GROUP * HD],
                                               start=(kd == 0), stop=(kd == KD - 1))
                    else:
                        for g in range(GROUPS):
                            mm = pe.matmul(misc[:, 0:D], oT[:, g, k * P:(k + 1) * P], wo[:, g, :],
                                           start=(g == 0), stop=(g == GROUPS - 1))
                    mm.then_inc(s_m, 1)

                row = [0]

                def tiles_before(at):
                    return row[0]

                def scores(b, u, j, ready):
                    g, i = divmod(u, TB)
                    if ready is not None:
                        pe.wait_ge(s_ex, ready)
                    pe.matmul(sc[j][:, i * P:(i + 1) * P], identb[:], mask[:], start=True, stop=False,
                              skip_group_check=True)
                    rows = slice(j * HP, (j + 1) * HP)
                    pe.matmul(sc[j][:, 0:(i + 1) * P], qT[g % 2][rows, i * P:(i + 1) * P],
                              kT[g % 2][rows, 0:(i + 1) * P], start=False, stop=True,
                              skip_group_check=True).then_inc(s_sc, 1)

                def turn_pv(b, u, between):
                    g, i = divmod(u, TB)
                    pe.wait_ge(s_ex, (b * UNITS + u) * GROUP + GROUP)

                    def pv(kt):
                        wait_read(pe, b, TURNS[u] + kt)
                        if kt == 0:
                            pe.wait_ge(s_at, b * UNITS + u + 1)
                        for j in range(GROUP):
                            mm = pe.matmul(o_ps[j * HP:(j + 1) * HP, :], v[g % 2][:, kt, j, :],
                                           probT[(PVS[u] + kt) % RT][:, j, :], start=(kt == 0), stop=(kt == i))
                        mm.then_inc(s_pv, 1)

                    for kt in range(i + 1):
                        q = TURNS[u] + kt
                        wait_read(pe, b, q - 2)
                        for j in range(GROUP):
                            mm = pe.transpose(turn[q % 2][:, j * P:(j + 1) * P],
                                              prob[u % 2][:, j, kt * P:(kt + 1) * P], K["ident"])
                        mm.then_inc(s_t, 1)
                        if kt > 1:
                            pv(kt - 2)
                    q = TURNS[u] + i + 1
                    pe.wait_ge(s_ib, b * UNITS + u + 1)
                    wait_read(pe, b, q - 2)
                    pe.transpose(turn[q % 2][:, 0:P], inv_b[:].rearrange("p j r -> p (j r)"),
                                 K["ident"]).then_inc(s_t, 1)
                    between()
                    if i > 0:
                        pv(i - 1)
                    pv(i)

                pe.wait_ge(s_w, 112)
                for n, (_, kind, k) in enumerate(FIRST):
                    use(n, kind, k)
                pe.wait_ge(s_c, 2)
                pe.wait_ge(s_me, M0)
                for j in range(GROUP):
                    scores(0, 0, j, None)

                def body(b, has_next):
                    row[0] = (b + 1) * TB
                    for u in range(UNITS):
                        nxt = u + 1
                        if nxt < UNITS or has_next:
                            if nxt % TB == 0:
                                done = [n for n, (at, _, _) in enumerate(uses(has_next)) if at <= u - 1]
                                pe.wait_ge(s_me, b * MU + M0 + done[-1] + 1)
                            for j in range(GROUP):
                                scores(b, nxt % UNITS, j, (b * UNITS + u) * GROUP + j + 1)

                        def projections():
                            for n, (at, kind, k) in enumerate(uses(has_next)):
                                if at == u and kind in "QKV":
                                    use(b * MU + M0 + n, kind, k)

                        turn_pv(b, u, projections)
                        for n, (at, kind, k) in enumerate(uses(has_next)):
                            if at == u and kind not in "QKV":
                                if kind == "out" and k == 0:
                                    pe.wait_ge(s_at, (b + 1) * UNITS + 1)
                                use(b * MU + M0 + n, kind, k)

                rows_loop(pe, body)

            @blk.vector
            def _(dve):
                c = Chain(dve, s_chain)
                for k in range(2):
                    c.step(dve.memset(v[k][:], 0.0))
                layer_norm_stats(dve, c, x_sb, stats, mean, var)
                dve.sem_inc(s_var, 1)
                dve.sem_inc(s_td, 2)
                dve.sem_inc(s_pv, RT)
                dve.sem_inc(s_at, 1)
                dve.wait_ge(s_root, 1)
                layer_norm_rstd(dve, c, var, root, rstd, stats[:, :, 0])
                dve.wait_ge(s_w, 112)

                def norm(tile, m, at):
                    dve.wait_ge(s_m, at - 1 if m >= 2 else at - m)
                    dve.tensor_scalar(xn_t[m % 2][:],
                                      x_sb[:, ds(tile, 1), :].rearrange("p a d -> p (a d)"),
                                      mean[:, ds(tile, 1)], rstd[:, ds(tile, 1)],
                                      ALU.subtract, ALU.mult).then_inc(s_xn, 1)

                def read(at, kind, k, b):
                    if kind == "T":
                        return
                    dve.wait_ge(s_m, at + 1)
                    if kind == "Q":
                        dve.scalar_tensor_tensor(out=qT[k % 2][:], in0=misc[:], scalar=HD ** -0.5,
                                                 in1=q_bias[:, k, :], op0=ALU.mult, op1=ALU.add).then_inc(s_me, 1)
                    elif kind == "K":
                        dve.tensor_tensor(kT[k % 2][:], misc[:], k_bias[:, k, :], ALU.add).then_inc(s_me, 1)
                    elif kind == "V":
                        dve.tensor_copy(v[k % 2][:, :, :, 0:HD],
                                        misc[:, 0:TB * GROUP * HD].rearrange("p (m j d) -> p m j d", m=TB,
                                                                             j=GROUP)).then_inc(s_me, 1)
                    else:
                        x_row = x_sb[:, ds(b * TB + k, 1), :].rearrange("p a d -> p (a d)")
                        dve.tensor_tensor(x_row, x_row, misc[:, 0:D], ALU.add).then_inc(s_me, 1)

                def tops(b, u):
                    i = u % TB
                    for j in range(GROUP):
                        dve.wait_ge(s_sc, (b * UNITS + u) * GROUP + j + 1)
                        dve.tensor_reduce(top[u % 2][:, j:j + 1], sc[j][:, 0:(i + 1) * P], AX.X, ALU.max,
                                          negate=True).then_inc(s_top, 1)

                def inverse(b, u):
                    dve.wait_ge(s_ex, (b * UNITS + u) * GROUP + GROUP)
                    dve.reciprocal(inv[:], total[u % 2][:]).then_inc(s_inv, 1)
                    dve.wait_ge(s_inv, b * UNITS + u + 1)
                    dve.tensor_copy(inv_b[:], inv[:].unsqueeze(2).broadcast_to([P, GROUP, HP])).then_inc(s_ib, 1)

                def turned(b, u):
                    g, i = divmod(u, TB)
                    for kt in [kt for kt in range(i + 1) if kt not in ACT_TILES]:
                        q = TURNS[u] + kt
                        dve.wait_ge(s_t, b * NTURN + q + 1)
                        dve.wait_ge(s_pv, b * NPV + PVS[u] + kt + 1)
                        dve.tensor_copy(probT[(PVS[u] + kt) % RT][:].rearrange("p j t -> p (j t)"),
                                        turn[q % 2][:]).then_inc(s_td, 1)
                    q = TURNS[u] + i + 1
                    dve.wait_ge(s_t, b * NTURN + q + 1)
                    dve.tensor_copy(inv_t[:], turn[q % 2][:, 0:P]).then_inc(s_td, 1)
                    wait_read(dve, b, q)
                    dve.wait_ge(s_pv, b * NPV + PVS[u] + i + 1 + RT)
                    if g == 0:
                        dve.wait_ge(s_m, b * MU + M0)
                    dve.tensor_tensor(oT[:, g, i * P:(i + 1) * P], o_ps[:], inv_t[:], ALU.mult).then_inc(s_at, 1)

                for n, (_, kind, k) in enumerate(FIRST):
                    if kind == "T":
                        norm(k, k, n)
                for n, (_, kind, k) in enumerate(FIRST):
                    read(n, kind, k, 0)
                tops(0, 0)

                def body(b, has_next):
                    for u in range(UNITS):
                        inverse(b, u)
                        if u < UNITS - 1:
                            tops(b, u + 1)
                        elif has_next:
                            tops(b + 1, 0)
                        turned(b, u)
                        for n, (at, kind, k) in enumerate(uses(has_next)):
                            if at == u and kind == "T":
                                norm((b + 1) * TB + k, k, b * MU + M0 + n)
                        for n, (at, kind, k) in enumerate(uses(has_next)):
                            if at == u:
                                read(b * MU + M0 + n, kind, k, b)

                rows_loop(dve, body)




def macaron_kernel(nc, A, out):
    with ExitStack() as ctx:
        x_sb = ctx.enter_context(nc.sbuf_tensor("x_sb", [P, NT, D], F32))
        ident = ctx.enter_context(nc.sbuf_tensor("ident", [P, P], F32))
        K = {"ident": ident[:], "routing": A["routing"]}
        xs = nc.dram_tensor("rows_by_slot", [slot_tiles(E0) * P, D], F32).ap()
        ys = nc.dram_tensor("results_by_slot", [slot_tiles(E0) * P, D], F32).ap()
        experts = {k: A["m0_" + k] for k in ("wgu", "wdn", "wr", "bgu", "bdn")}
        with_shared = {k: A["m1_" + k] for k in ("wgu", "wdn", "wr", "ebias", "wsgu", "wsdn")}

        s_x = nc.alloc_semaphore("x_in")
        with nc.Block() as blk:
            @blk.sync
            def _(sp):
                sp.dma_start(x_sb[:], A["x"].rearrange("(i p) d -> p i d", p=P)).then_inc(s_x, 16)
                sp.dma_start(ident[:], A["ident"]).then_inc(s_x, 16)
                sp.wait_ge(s_x, 32)

        with nc.cleanup_on_exit():
            moe_phase(nc, "ffn0", x_sb, K, xs, ys, experts, E0, False, clear=True)
        with nc.cleanup_on_exit():
            mamba_phase(nc, x_sb, K, A)
        with nc.cleanup_on_exit():
            moe_phase(nc, "ffn1", x_sb, K, xs, ys, experts, E0, False)
        with nc.cleanup_on_exit():
            moe_phase(nc, "ffn2", x_sb, K, xs, ys, with_shared, E1, True)
        with nc.cleanup_on_exit():
            attention_phase(nc, x_sb, K, A)
        with nc.cleanup_on_exit():
            moe_phase(nc, "ffn3", x_sb, K, xs, ys, with_shared, E1, True, out=out)


def laid_out(np, inputs):
    g = {k: np.asarray(v) for k, v in inputs.items()}
    rows = lambda a: np.ascontiguousarray(
        a.reshape(a.shape[0] // P, P, a.shape[1]).transpose(1, 0, 2))
    A = {"x": g["L0_attn_input"].reshape(T, D)}
    gu = g["L0_ffn_gate_up_proj"]
    split = lambda a: np.concatenate([a[..., ::2], a[..., 1::2]], axis=-1)
    by_expert = lambda a: np.ascontiguousarray(
        a.reshape(a.shape[0], a.shape[1] // P, P, a.shape[2]).transpose(2, 1, 0, 3))
    A["m0_wgu"] = by_expert(split(gu))
    A["m0_wdn"] = by_expert(g["L0_ffn_down_proj"])[:, 0]
    A["m0_wr"] = rows(g["L0_ffn_router_weight"])
    A["m0_bgu"] = split(g["L0_ffn_gate_up_proj_bias"])
    A["m0_bdn"] = g["L0_ffn_down_proj_bias"]
    A["m1_wgu"] = by_expert(np.concatenate([g["L1_ffn_Wg"], g["L1_ffn_Wu"]], axis=-1))
    A["m1_wdn"] = by_expert(g["L1_ffn_Wd"])[:, 0]
    A["m1_wr"] = rows(g["L1_ffn_Wr"])
    A["m1_ebias"] = g["L1_ffn_expert_bias"]
    A["m1_wsgu"] = rows(np.concatenate([g["L1_ffn_Sg"], g["L1_ffn_Su"]], axis=-1))
    A["m1_wsdn"] = rows(g["L1_ffn_Sd"])
    win, b_in = g["L0_attn_Win"].T, g["L0_attn_b_in"]
    A["ssm_win"] = rows(np.ascontiguousarray(win[:, :2 * CH]))
    gap = lambda a: np.concatenate([a[..., :NS], np.zeros((*a.shape[:-1], RANK - NS), np.float32),
                                    a[..., NS:]], axis=-1)
    A["ssm_wbd"] = rows(gap(win[:, 2 * CH:]))
    A["ssm_wdt"] = np.concatenate([np.zeros((RANK, CH), np.float32), g["L0_attn_Wdt"].T])
    A["ssm_wout"] = rows(g["L0_attn_Wout"].T)
    blocks = lambda a: a.reshape(-1, P).T
    b_param = np.concatenate([g["L0_attn_B_param"], np.zeros(P - NS, np.float32)])
    A["ssm_col"] = np.concatenate(
        [blocks(b_in[:2 * CH]), blocks(g["L0_attn_b_dt"]), blocks(gap(b_in[2 * CH:])), blocks(b_param),
         g["L0_attn_Wconv"].reshape(CB, P, TAPS).transpose(1, 0, 2).reshape(P, CB * TAPS)], axis=1)
    A["ssm_alog"] = g["L0_attn_A_log"].reshape(CB, P, NS).transpose(1, 0, 2)
    A["ssm_cmat"] = g["L0_attn_C_param"].reshape(CB, P, NS).transpose(1, 0, 2)
    A["ssm_bout"] = g["L0_attn_b_out"]
    def spaced(a):
        out = np.zeros((a.shape[0], HEADS, HP), np.float32)
        out[:, :, :HD] = a.reshape(a.shape[0], HEADS, HD)
        return out.reshape(a.shape[0], HEADS * HP)
    A["att_wq"] = rows(spaced(g["L1_attn_W_Q"].T))
    A["att_wk"] = rows(spaced(g["L1_attn_W_K"].T))
    A["att_wv"] = rows(g["L1_attn_W_V"].T)
    A["att_wo"] = rows(np.ascontiguousarray(spaced(g["L1_attn_W_O"]).T))
    slope = (1.0 / (2.0 ** 8) ** ((np.arange(HEADS, dtype=np.float32) + 1) / HEADS)).astype(np.float32)
    place = (np.arange(SEQ) - SEQ // 2).astype(np.float32)
    q_bias, k_bias = (np.zeros((GROUPS, GROUP, HP, SEQ), np.float32) for _ in range(2))
    steep = slope.reshape(GROUPS, GROUP)[:, :, None] * place
    q_bias[:, :, HD], k_bias[:, :, HD] = 1.0, steep
    q_bias[:, :, HD + 1], k_bias[:, :, HD + 1] = -steep, 1.0
    for name, a in (("att_q_bias", q_bias), ("att_k_bias", k_bias)):
        A[name] = a.transpose(1, 2, 0, 3).reshape(P, GROUPS, SEQ)
    q = np.arange(P)
    A["att_mask"] = np.where(q[None, :] <= q[:, None], 0.0, MASKED).astype(np.float32)
    p = np.arange(P)
    consts = {
        "before": p[:, None] < p[None, :], "ones": np.ones((P, P)),
        "e_less": np.broadcast_to(np.arange(E0) - 64, (P, E0)),
        "restart": np.broadcast_to((np.arange(E0 * NT) % NT) > 0, (P, E0 * NT)),
        "tile_start": np.broadcast_to(np.arange(NT) * P, (P, NT)),
        "j": np.broadcast_to(np.arange(slot_tiles(E0)), (P, slot_tiles(E0))),
    }
    A["routing"] = np.concatenate([consts[k].astype(np.float32) for k in ROUTING], axis=1)
    A["ident"] = np.eye(P, dtype=np.float32)
    A = {k: np.ascontiguousarray(v) for k, v in A.items()}
    return A


def kernel(**inputs):
    import numpy as _np
    import concourse.bacc as _bacc
    from concourse import mybir as _mybir
    from concourse.bass_utils import run_bass_kernel_spmd as _run

    nc = _bacc.Bacc("TRN2", target_bir_lowering=False, num_devices=1)
    arrays = {f"in_{k}_dram": v for k, v in laid_out(_np, inputs).items()}
    args = {k[3:-5]: nc.dram_tensor(k, a.shape, _mybir.dt.from_np(a.dtype), kind="ExternalInput").ap()
            for k, a in arrays.items()}
    out = nc.dram_tensor("out_0_dram", (T, D), _mybir.dt.float32, kind="ExternalOutput").ap()
    macaron_kernel(nc, args, out)
    r = _run(nc, [arrays], core_ids=[0])
    return r.results[0]["out_0_dram"].reshape(BATCH, SEQ, D)
```
